# Optimizing a Trainium2 kernel written in Bass

```python
import numpy as np
import jax
import jax.numpy as jnp

def _softmax(x, axis=-1):
    return jax.nn.softmax(x, axis=axis)

def _gelu(x):
    return jax.nn.gelu(x, approximate=True)

def _silu(x):
    return jax.nn.silu(x)

def _sigmoid(x):
    return jax.nn.sigmoid(x)

def _layernorm(x, axis=-1, eps=1e-05):
    m = jnp.mean(x, axis=axis, keepdims=True)
    v = jnp.var(x, axis=axis, keepdims=True)
    return (x - m) / jnp.sqrt(v + eps)

def _scatter_add(tgt, idx, src, axis=0):
    return tgt.at[idx].add(src)

def _segment_sum(src, seg, n):
    return jax.ops.segment_sum(src, seg, n)
kernel_name = 'mk_seq_postln_d1_jaxref_r4_cf3726'

def setup_inputs(seed: int=0):
    np.random.seed(seed)
    _w = jnp.asarray

    def _L0_attn_setup():
        import jax, jax.numpy as jnp
        import numpy as np
        import math
        D_MODEL = 256
        N_HEADS = 16
        D_HEAD = D_MODEL // N_HEADS
        key = jax.random.key(seed)
        k1, k2, k3 = jax.random.split(key, 3)
        x = jax.random.normal(k1, (4, 512, D_MODEL), dtype=jnp.float32)
        s = 1.0 / math.sqrt(D_MODEL)
        W_qkv = jax.random.uniform(k2, (3 * D_MODEL, D_MODEL), jnp.float32, -s, s)
        W_proj = jax.random.uniform(k3, (D_MODEL, D_MODEL), jnp.float32, -s, s)
        return {'x': x, 'W_qkv': W_qkv, 'W_proj': W_proj}
    _L0_attn_in = _L0_attn_setup()

    def _L0_ffn_setup():
        import jax, jax.numpy as jnp
        import numpy as np
        DIM = 256
        HIDDEN = 768
        SCALE = 1.0 / 127.0

        def _dequant(w_int, dtype):
            return w_int.astype(dtype) * jnp.asarray(SCALE, dtype)
        key = jax.random.key(seed)
        k_x, k_g, k_u, k_d = jax.random.split(key, 4)
        x = jax.random.normal(k_x, (4, 512, DIM), dtype=jnp.float32)
        w_gate = jax.random.randint(k_g, (HIDDEN, DIM), -127, 128, dtype=jnp.int32)
        w_up = jax.random.randint(k_u, (HIDDEN, DIM), -127, 128, dtype=jnp.int32)
        w_down = jax.random.randint(k_d, (DIM, HIDDEN), -127, 128, dtype=jnp.int32)
        return {'x': x, 'w_gate': w_gate, 'w_up': w_up, 'w_down': w_down}
    _L0_ffn_in = _L0_ffn_setup()
    _d = {'L0_attn_x': _L0_attn_in['x'], 'L0_attn_W_qkv': _L0_attn_in['W_qkv'], 'L0_attn_W_proj': _L0_attn_in['W_proj'], 'L0_ffn_w_gate': _L0_ffn_in['w_gate'], 'L0_ffn_w_up': _L0_ffn_in['w_up'], 'L0_ffn_w_down': _L0_ffn_in['w_down']}
    _x0 = _d['L0_attn_x']
    _d['L0_attn_x'] = jax.random.normal(jax.random.fold_in(jax.random.key(seed), 1), (8, 1024, 256), dtype=_x0.dtype)
    del _x0
    return _d

def reference(L0_attn_x, L0_attn_W_qkv, L0_attn_W_proj, L0_ffn_w_gate, L0_ffn_w_up, L0_ffn_w_down):

    def _L0_attn_ref(x, W_qkv, W_proj):
        import jax, jax.numpy as jnp
        import numpy as np
        import math
        D_MODEL = 256
        N_HEADS = 16
        D_HEAD = D_MODEL // N_HEADS
        B, T, d = x.shape
        qkv = x @ W_qkv.T
        q, k, v = jnp.split(qkv, 3, axis=-1)

        def split(t):
            return t.reshape(B, T, N_HEADS, D_HEAD).transpose(0, 2, 1, 3)
        q, k, v = (split(q), split(k), split(v))
        scores = jnp.einsum('bhqd,bhkd->bhqk', q, k) / math.sqrt(D_HEAD)
        mask = jnp.tril(jnp.ones((T, T), dtype=bool))
        scores = jnp.where(mask, scores, -jnp.inf)
        attn = jax.nn.softmax(scores, axis=-1)
        out = jnp.einsum('bhqk,bhkd->bhqd', attn, v)
        out = out.transpose(0, 2, 1, 3).reshape(B, T, d)
        return out @ W_proj.T

    def _L0_ffn_ref(x, w_gate, w_up, w_down):
        import jax, jax.numpy as jnp
        import numpy as np
        DIM = 256
        HIDDEN = 768
        SCALE = 1.0 / 127.0

        def _dequant(w_int, dtype):
            return w_int.astype(dtype) * jnp.asarray(SCALE, dtype)
        wg = _dequant(w_gate, x.dtype)
        wu = _dequant(w_up, x.dtype)
        wd = _dequant(w_down, x.dtype)
        gate = jnp.einsum('bsd,hd->bsh', x, wg)
        up = jnp.einsum('bsd,hd->bsh', x, wu)
        h = jax.nn.silu(gate) * up
        return jnp.einsum('bsh,dh->bsd', h, wd)
    x = L0_attn_x
    x = _layernorm(x + _L0_attn_ref(x, L0_attn_W_qkv, L0_attn_W_proj), axis=-1)
    x = _layernorm(x + _L0_ffn_ref(x, L0_ffn_w_gate, L0_ffn_w_up, L0_ffn_w_down), axis=-1)
    return x

_drawn_inputs = setup_inputs


def setup_inputs(seed=0):
    import zlib

    import numpy as np

    out = dict(_drawn_inputs(seed))
    spreads = {}
    factors = {}
    for name, (base, spread) in spreads.items():
        noise = np.random.default_rng([zlib.crc32(name.encode()), seed]).standard_normal(out[name].shape)
        drawn = base * np.exp(spread * noise) if base else spread * noise
        out[name] = jnp.asarray(drawn.astype(out[name].dtype))
    for name, factor in factors.items():
        out[name] = (out[name] * factor).astype(out[name].dtype)
    return out
```

```python
from contextlib import ExitStack

import concourse.bass as bass
from concourse import mybir

F32 = mybir.dt.float32
BF16 = mybir.dt.bfloat16
F16 = mybir.dt.float16
I32 = mybir.dt.int32
ALU = mybir.AluOpType
ACT = mybir.ActivationFunctionType


def attention_steps(slots, diagonal, max_items, ahead, has_max, has_m, has_st):
    COLS, EXP, ROW_MAX, MASK, PV, COPY, HANDOVER = 54, (60, 107), (75, 134), 620, 235, 490, 100
    ns, nm, hg = len(slots), len(max_items), 4
    whole, whole_max = hg * sum(w for _, _, w in slots), sum(max_items)
    pe = act = dve = pool = o_free = 0
    st_free, s_free = [0, 0], [0, 0]
    pv_ready = {s: 0 for s in range(ahead)}
    n, end, m, p = hg * ahead, hg * (ns + ahead * has_st), 0, 0
    st_cols = max_cols = pv_cols = 0
    turns, order = [], []
    while n < end or p < ns or turns or (has_max and m < nm):
        could = []
        if n < end and n // hg < p + 3:
            could.append((st_free[n % 2], st_cols / whole, "st"))
        if has_max and m < nm:
            could.append((s_free[m % 2], max_cols / whole_max, "max"))
        if p < ns and p in pv_ready:
            could.append((max(pv_ready[p], o_free if slots[p][1] == 0 else 0), pv_cols / whole, "pv"))
        if turns:
            could.append((turns[0][1], 2, "oT"))
        ready = [c for c in could if c[0] <= pe] or [min(could)]
        start, _, what = min(ready, key=lambda c: c[1])
        pe = max(pe, start)
        if what == "st":
            s, j = divmod(n, hg)
            w = slots[s % ns][2]
            order.append(("st", s, j))
            pe += w * COLS
            act = max(act, pe + HANDOVER) + EXP[0] + w * EXP[1]
            st_free[n % 2] = act + HANDOVER
            n, st_cols = n + 1, st_cols + w
            if j == hg - 1:
                pv_ready[s] = act + HANDOVER
                if s % ns in diagonal:
                    pool = max(pool, act + HANDOVER) + MASK
                    pv_ready[s] = pool + HANDOVER
            if n == hg * (ahead + 1) and has_m:
                order.append(("mT",))
        elif what == "max":
            order.append(("max", m))
            pe += max_items[m] * COLS
            dve = max(dve, pe + HANDOVER) + ROW_MAX[0] + max_items[m] * ROW_MAX[1]
            s_free[m % 2] = dve + HANDOVER
            m, max_cols = m + 1, max_cols + max_items[m]
        elif what == "pv":
            order.append(("pv", p))
            pe += slots[p][2] * PV
            p, pv_cols = p + 1, pv_cols + hg * slots[p][2]
            if p == ns or slots[p][0] != slots[p - 1][0]:
                half = slots[p - 1][0]
                order.append(("oC", half))
                act = max(act, pe + HANDOVER) + COPY
                o_free = act + HANDOVER
                turns.append((half, o_free))
        else:
            order.append(("oT", turns.pop(0)[0]))
            pe += COPY
            dve = max(dve, pe + HANDOVER) + COPY
    return order


def block_kernel(nc, x, w_qkv, w_proj, w_gate, w_up, w_down, out):
    P = 128
    B, T, D = x.shape
    HID = w_gate.shape[0]
    H = 16
    DH = D // H
    NTOK = B * T
    CH = 512
    NCH = NTOK // CH
    TILES = CH // P
    KC = D // P
    HC = HID // P
    QT = T // P
    HG = 4
    NG = H // HG
    GROUPS = B * NG
    EPS = 1e-5
    SOFT_SCALE = 1.0 / float(DH) ** 0.5
    W_SCALE = 1.0 / 127.0
    LOWEST = -3.0e38
    PAIRS = [(0, 0), (1, 0), (2, 0), (0, 1), (1, 1), (0, 2)]
    ROWS = len(PAIRS) * DH
    ROWS_M = ROWS + 3

    HQ = QT // 2
    slots = [(0, kt, HQ - kt) for kt in range(HQ)]
    slots += [(1, kt, min(HQ, QT - kt)) for kt in range(QT)]
    diagonal = [s for s, (half, kt, w) in enumerate(slots) if kt >= half * HQ]
    NS = len(slots)
    NE = NS * HG
    NM = HG * QT
    ND = len(diagonal)
    max_items = [qt + 1 for j in range(HG) for qt in range(QT)]
    HALF_END = [HQ - 1, NS - 1]
    AHEAD = 2

    xf = x.rearrange("b t d -> (b t) d")
    of = out.rearrange("b t d -> (b t) d")
    x_tiles = xf.rearrange("(c p) d -> p c d", p=P)
    out_tiles = of.rearrange("(c p) d -> p c d", p=P)
    qk_dram = nc.dram_tensor("qk_parts", [2, 3, D, NTOK], BF16, kind="Internal").ap()
    v_dram = nc.dram_tensor("v_rows", [NTOK, D], F32, kind="Internal").ap()
    a_dram = nc.dram_tensor("attn_rows", [NTOK, D], F32, kind="Internal").ap()
    v_tiles = v_dram.rearrange("(c p) d -> p c d", p=P)
    a_tiles = a_dram.rearrange("(c p) d -> p c d", p=P)

    with ExitStack() as ctx:
        def sb(name, shape, dt):
            return ctx.enter_context(nc.sbuf_tensor(name, shape, dt))

        def sem(name):
            return ctx.enter_context(nc.semaphore(name))

        ps = ctx.enter_context(nc.psum_tensor("ps", [P, 8, 512], F32))

        ident = sb("ident", [P, P], F32)
        ident_bf = sb("ident_bf", [P, P], BF16)
        causal = sb("causal", [P, T], F32)
        minus_half = sb("minus_half", [P, TILES], F32)
        wqkv_t = sb("wqkv_t", [P, KC, 3 * D], F32)
        wproj_t = sb("wproj_t", [P, KC, D], F32)
        wgate_t = sb("wgate_t", [P, KC, HID], BF16)
        wup_t = sb("wup_t", [P, KC, HID], BF16)
        wdown_t = sb("wdown_t", [P, HC, D], BF16)

        x_sb = [sb(f"x_sb{i}", [P, TILES, D], F32) for i in range(2)]
        x_t = [sb(f"x_t{i}", [P, KC, CH], F32) for i in range(2)]
        parts = [sb(f"parts{i}", [P, 3, CH], BF16) for i in range(4)]
        rest = [sb(f"rest{i}", [P, CH], F32) for i in range(2)]
        v_sb = [sb(f"v_sb{i}", [P, TILES, D], F32) for i in range(2)]
        with ExitStack() as early:
            def sb_early(name, shape, dt):
                return early.enter_context(nc.sbuf_tensor(name, shape, dt))

            wqkv_n = sb_early("wqkv_n", [P, 3 * KC, D], F32)
            wproj_n = sb_early("wproj_n", [P, KC, D], F32)
            wgate_n = sb_early("wgate_n", [P, HC, D], I32)
            wup_n = sb_early("wup_n", [P, HC, D], I32)
            wdown_n = sb_early("wdown_n", [P, KC, HID], I32)
            wgate_b = sb_early("wgate_b", [P, HC, D], BF16)
            wup_b = sb_early("wup_b", [P, HC, D], BF16)
            wdown_b = sb_early("wdown_b", [P, KC, HID], BF16)

        with ExitStack() as middle:
            def sb_middle(name, shape, dt):
                return middle.enter_context(nc.sbuf_tensor(name, shape, dt))

            q_stack = [sb_middle(f"q_stack{i}", [P, HG, T], BF16) for i in range(4)]
            v_flat = [sb_middle(f"v_flat{i}", [P, QT, HG * DH], F32) for i in range(2)]
            k_stack = [sb_middle(f"k_stack{i}", [P, HG, T], BF16) for i in range(4)]
            v_ones = [sb_middle(f"v_ones{i}", [P, QT, HG, 32], F32) for i in range(2)]
            probs = [sb_middle(f"probs{i}", [P, HG, CH], F32) for i in range(3)]
            row_max = sb_middle("row_max", [P, NM], F32)
            max_rest = sb_middle("max_rest", [P, 2, NM], F32)
            max_parts = sb_middle("max_parts", [P, 3, NM], BF16)
            max_rows = sb_middle("max_rows", [3 * NM, P], BF16)
            o_sb = sb_middle("o_sb", [P, CH], F32)
            recip = sb_middle("recip", [P, HQ, HG], F32)
            attn_sb = [sb_middle(f"attn_sb{i}", [P, HQ, HG, DH], F32) for i in range(2)]

        a_sb = v_sb
        a_t = x_t[0]
        x1 = [sb(f"x1_{i}", [P, TILES, D], F32) for i in range(2)]
        x1_hi = sb("x1_hi", [P, KC, CH], F16)
        x1_lo = sb("x1_lo", [P, KC, CH], F16)
        silu = [sb(f"silu{i}", [P, CH], F32) for i in range(2)]
        h_sb = [sb(f"h_sb{i}", [P, CH], F32) for i in range(3)]
        h_hi = sb("h_hi", [P, HC, CH], F16)
        h_lo = sb("h_lo", [P, HC, CH], F16)
        z_sb = [sb(f"z_sb{i}", [P, TILES, D], F32) for i in range(2)]
        stats = sb("stats", [P, 2, TILES, 6], F32)
        mean_var = sb("mean_var", [P, 2, TILES, 2], F32)
        var_eps = sb("var_eps", [P, 2, TILES], F32)
        rstd = sb("rstd", [P, 2, TILES], F32)

        w_loaded = {n: sem(f"w_loaded_{n}") for n in ("qkv", "proj", "gate", "up", "down")}
        consts_ready = sem("consts_ready")
        preset = sem("preset")
        w_cast = sem("w_cast")
        wt_ready = sem("wt_ready")
        wt_copied = [sem("wt_copied_act"), sem("wt_copied_dve")]
        dve_passed = sem("dve_passed")
        pool_passed = sem("pool_passed")
        sp_passed = sem("sp_passed")
        x_loaded = [sem(f"x_loaded{i}") for i in range(2)]
        xt_ready = sem("xt_ready")
        xt_copied = [sem("xt_copied_act"), sem("xt_copied_dve")]
        qk_ready = sem("qk_ready")
        part0_done = sem("part0_done")
        qk_bank_free = sem("qk_bank_free")
        part1_done = sem("part1_done")
        part2_done = sem("part2_done")
        parts_stored = [sem(f"parts_stored{i}") for i in range(4)]
        v_ready = sem("v_ready")
        v_copied = [sem("v_copied_act"), sem("v_copied_dve")]
        v_stored = [sem(f"v_stored{i}") for i in range(2)]
        stack_loaded = [sem(f"stack_loaded{i}") for i in range(4)]
        v_loaded = [sem(f"v_loaded{i}") for i in range(2)]
        v_expanded = sem("v_expanded")
        s_ready = sem("s_ready")
        s_free = sem("s_free")
        max_step = sem("max_step")
        max_parts_ready = sem("max_parts_ready")
        max_turned = sem("max_turned")
        max_rows_loaded = sem("max_rows_loaded")
        st_ready = sem("st_ready")
        exp_done = sem("exp_done")
        masked = sem("masked")
        pv_done = sem("pv_done")
        o_copied = sem("o_copied")
        o_turned = sem("o_turned")
        recip_done = sem("recip_done")
        turn_free = sem("turn_free")
        attn_stored = [sem(f"attn_stored{i}") for i in range(2)]
        xa_loaded = [sem(f"xa_loaded{i}") for i in range(2)]
        at_ready = sem("at_ready")
        at_copied = [sem("at_copied_act"), sem("at_copied_dve")]
        proj_ready = sem("proj_ready")
        y_done = sem("y_done")
        ln1_step = sem("ln1_step")
        rstd_done = [sem("rstd1_done"), sem("rstd2_done")]
        x1_ready = sem("x1_ready")
        x1t_ready = sem("x1t_ready")
        x1_hi_done = sem("x1_hi_done")
        x1_lo_done = sem("x1_lo_done")
        gate_ready = sem("gate_ready")
        up_ready = sem("up_ready")
        silu_done = sem("silu_done")
        h_done = sem("h_done")
        h_hi_done = sem("h_hi_done")
        h_lo_done = sem("h_lo_done")
        down_ready = sem("down_ready")
        z_done = sem("z_done")
        ln2_step = sem("ln2_step")
        out_ready = sem("out_ready")
        out_stored = [sem(f"out_stored{i}") for i in range(2)]

        def bank_bf(b):
            return ps[:, b, :].bitcast(BF16)

        units = []
        for kc in range(KC):
            for r in (0, 3):
                units.append(("qkv", [wqkv_n[:, r + i, kc * P:(kc + 1) * P] for i in range(3)],
                              wqkv_t[:, kc, r * P:(r + 3) * P]))
        for kc in range(KC):
            units.append(("proj", [wproj_n[:, r, kc * P:(kc + 1) * P] for r in range(KC)], wproj_t[:, kc, :]))
        for name, src, dst in (("gate", wgate_b, wgate_t), ("up", wup_b, wup_t)):
            for kc in range(KC):
                for r in (0, 3):
                    units.append((name, [src[:, r + i, kc * P:(kc + 1) * P] for i in range(3)],
                                  dst[:, kc, r * P:(r + 3) * P]))
        for hc in range(0, HC, 2):
            units.append(("down", [wdown_b[:, r, (hc + i) * P:(hc + i + 1) * P] for i in range(2) for r in range(KC)],
                          wdown_t[:, hc:hc + 2, :].rearrange("p a b -> p (a b)")))
        casts = {"gate": 1, "up": 2, "down": 3}

        def unit_bank(u):
            name, tiles, dst = units[u]
            bank = bank_bf(u % 8) if name in casts else ps[:, u % 8, :]
            return bank[:, 0:len(tiles) * P]

        PAIRS_LOOPED = NCH // 2 - 1

        def tile_cols(t):
            return slice(t * P, (t + 1) * P)

        def group_steps(b_last, g):
            return attention_steps(slots, diagonal, max_items, AHEAD, not (b_last and g >= NG - 2),
                                   not (b_last and g == NG - 1), not (b_last and g == NG - 1))

        def at(b, g, per, n):
            return b * (NG * per) + (g * per + n)

        def turn_use(b, g, b_last, k):
            skipped = 1 if b_last and g == 3 else 0
            return at(b, g, 3, 1 + k - (skipped if k else 0))

        block = ctx.enter_context(nc.Block())

        @block.sync
        def _(sp):
            sp.dma_start(wqkv_n[:], w_qkv.rearrange("(r p) d -> p r d", p=P)).then_inc(w_loaded["qkv"], 16)
            for c in range(2):
                sp.dma_start(x_sb[c][:], x_tiles[:, c * TILES:(c + 1) * TILES, :]).then_inc(x_loaded[c], 16)
            sp.dma_start(wproj_n[:], w_proj.rearrange("(r p) d -> p r d", p=P)).then_inc(w_loaded["proj"], 16)
            sp.dma_start(wgate_n[:], w_gate.rearrange("(r p) d -> p r d", p=P)).then_inc(w_loaded["gate"], 16)
            sp.dma_start(wup_n[:], w_up.rearrange("(r p) d -> p r d", p=P)).then_inc(w_loaded["up"], 16)
            sp.dma_start(wdown_n[:], w_down.rearrange("(r p) d -> p r d", p=P)).then_inc(w_loaded["down"], 16)

            def chunk_a(c, i, par, load):
                if load:
                    sp.wait_ge(xt_ready, 2 * c + 2)
                    sp.dma_start(x_sb[par][:], x_tiles[:, bass.ds((c + 2) * TILES, TILES), :]).then_inc(x_loaded[par], 16)
                for m in range(4):
                    sp.wait_ge(part2_done, 4 * c + 2 + m + 1)
                    sp.dma_start(
                        qk_dram[m // 2, :, (m % 2) * P:(m % 2 + 1) * P, bass.ds(c * CH, CH)].rearrange("w r t -> r w t"),
                        parts[m][:]).then_inc(parts_stored[m], 16)
                sp.wait_ge(v_copied[0], c + 2)
                sp.wait_ge(v_copied[1], c + 2)
                sp.dma_start(v_tiles[:, bass.ds(c * TILES, TILES), :], v_sb[par][:]).then_inc(v_stored[par], 16)

            with sp.Fori(0, PAIRS_LOOPED) as i:
                for par in range(2):
                    chunk_a(2 * i + par, i, par, True)
            for par in range(2):
                chunk_a(2 * PAIRS_LOOPED + par, PAIRS_LOOPED, par, False)

            def load_stacks(b, g):
                for r, pair in enumerate(PAIRS):
                    for which, stack in ((0, q_stack), (1, k_stack)):
                        src = qk_dram[which, pair[which], g * HG * DH:(g + 1) * HG * DH, bass.ds(b * T, T)]
                        sp.dma_start(stack[g][r * DH:(r + 1) * DH, :, :],
                                     src.rearrange("(j r) t -> r j t", j=HG)).then_inc(stack_loaded[g], 16)

            def load_v(b, g):
                sp.dma_start(v_flat[g % 2][:], v_tiles[:, bass.ds(b * QT, QT), g * HG * DH:(g + 1) * HG * DH]
                             ).then_inc(v_loaded[g % 2], 16)

            def load_max_rows(g):
                for part in range(3):
                    sp.dma_start(q_stack[g][ROWS + part:ROWS + part + 1, :, :].rearrange("p j (t c) -> p (j t) c", c=P),
                                 max_rows[part * NM:(part + 1) * NM, :]).then_inc(max_rows_loaded, 16)

            def store_attn(b, g, b_last, half):
                sp.wait_ge(turn_free, turn_use(b, g, b_last, 1 + half) + 2)
                sp.sem_inc(sp_passed, 1)
                sp.dma_start(a_tiles[:, bass.ds(b * QT + half * HQ, HQ), g * HG * DH:(g + 1) * HG * DH],
                             attn_sb[half][:].rearrange("p t j d -> p t (j d)")).then_inc(attn_stored[half], 16)

            for m in range(4):
                sp.wait_ge(parts_stored[m], 16 * (NCH + 1))
            for par in range(2):
                sp.wait_ge(v_stored[par], 16 * (NCH // 2 + 1))
            load_stacks(0, 0)
            load_v(0, 0)
            load_stacks(0, 1)
            load_v(0, 1)
            load_stacks(0, 2)
            sp.wait_ge(turn_free, 2)
            load_max_rows(0)

            def group_b(b, g, b_last):
                nb, ng = (b + 1, g + 3 - NG) if g + 3 >= NG else (b, g + 3)
                if not (b_last and g + 3 >= NG):
                    sp.wait_ge(pv_done, at(b, g, NS, 3))
                    load_stacks(nb, ng)
                if not (b_last and g + 2 >= NG):
                    sp.wait_ge(v_expanded, at(b, g, 1, 1))
                    load_v(b + 1 if g + 2 >= NG else b, (g + 2) % NG)
                if not (b_last and g + 1 >= NG):
                    sp.wait_ge(turn_free, turn_use(b, g, b_last, 0) + 2)
                    load_max_rows((g + 1) % NG)
                for half in range(2):
                    store_attn(b, g, b_last, half)

            with sp.Fori(0, B - 1) as b:
                for g in range(NG):
                    group_b(b, g, False)
            for g in range(NG):
                group_b(B - 1, g, True)

            for half in range(2):
                sp.wait_ge(attn_stored[half], 16 * (GROUPS + 1))

            def load_xa(c, par):
                sp.dma_start(x_sb[par][:], x_tiles[:, bass.ds(c * TILES, TILES), :]).then_inc(xa_loaded[par], 16)
                sp.dma_start(a_sb[par][:], a_tiles[:, bass.ds(c * TILES, TILES), :]).then_inc(xa_loaded[par], 16)

            load_xa(0, 0)
            load_xa(1, 1)

            def chunk_c(c, par, load):
                if load:
                    sp.wait_ge(y_done, 2 * c + 2)
                    load_xa(c + 2, par)
                sp.wait_ge(out_ready, c + 1)
                sp.dma_start(out_tiles[:, bass.ds(c * TILES, TILES), :], z_sb[par][:]).then_inc(out_stored[par], 16)

            with sp.Fori(0, PAIRS_LOOPED) as i:
                for par in range(2):
                    chunk_c(2 * i + par, par, True)
            for par in range(2):
                chunk_c(2 * PAIRS_LOOPED + par, par, False)
            for par in range(2):
                sp.wait_ge(out_stored[par], 16 * (NCH // 2 + 1))

        @block.gpsimd
        def _(pool):
            pool.memset(ident[:], 0.0).then_inc(consts_ready, 1)
            pool.memset(causal[:], 0.0).then_inc(consts_ready, 1)
            pool.memset(minus_half[:], -0.5)
            pool.wait_ge(consts_ready, 2)
            pool.affine_select(out=ident[:], in_=ident[:], compare_op=ALU.not_equal, fill=1.0, base=0,
                               pattern=[[-1, P]], channel_multiplier=1).then_inc(consts_ready, 1)
            pool.affine_select(out=causal[:, T - P:T], in_=causal[:, T - P:T], compare_op=ALU.is_ge, fill=LOWEST,
                               base=0, pattern=[[-1, P]], channel_multiplier=1).then_inc(consts_ready, 1)
            pool.wait_ge(consts_ready, 4)
            pool.tensor_copy(ident_bf[:], ident[:]).then_inc(consts_ready, 1)
            pool.wait_ge(consts_ready, 5)
            for i in range(2):
                pool.memset(v_ones[i][:, :, :, DH:32], 1.0).then_inc(preset, 1)
                pool.wait_ge(preset, i + 1)
            for g in range(4):
                pool.memset(k_stack[g][ROWS:ROWS_M, :, :], -1.0).then_inc(preset, 1)
                pool.wait_ge(preset, 2 + g + 1)

            def expand_v(b, g):
                pool.wait_ge(v_loaded[g % 2], 16 * (2 * b + g // 2 + 1))
                pool.sem_inc(pool_passed, 1)
                pool.tensor_copy(v_ones[g % 2][:, :, :, 0:DH],
                                 v_flat[g % 2][:].rearrange("p t (j d) -> p t j d", j=HG)).then_inc(v_expanded, 1)

            expand_v(0, 0)

            def mask(s, exps):
                pool.wait_ge(exp_done, exps + 2)
                pool.sem_inc(pool_passed, 1)
                tile = probs[s % 3][:, :, 0:P]
                pool.affine_select(out=tile, in_=tile, compare_op=ALU.is_ge, fill=0.0, base=0,
                                   pattern=[[0, HG], [1, P]], channel_multiplier=-1).then_inc(masked, 1)

            for s in range(AHEAD):
                mask(s, HG * (s + 1))

            def group_b(b, g, b_last):
                last_group = b_last and g == NG - 1
                for d, s in enumerate(s for s in range(AHEAD, NS if last_group else NS + AHEAD) if s % NS in diagonal):
                    if d == 1 and not last_group:
                        pool.wait_ge(pv_done, at(b, g, NS, 3))
                        expand_v(b + 1 if g == NG - 1 else b, (g + 1) % NG)
                    mask(s, at(b, g, NE, HG * (s + 1)))

            with pool.Fori(0, B - 1) as b:
                for g in range(NG):
                    group_b(b, g, False)
            for g in range(NG):
                group_b(B - 1, g, True)

            pool.sem_inc(h_lo_done, 3)

            def inverse_deviation(ln, step, c):
                pool.wait_ge(step, 3 * c + 3)
                pool.tensor_tensor(rstd[:, ln, :], var_eps[:, ln, :], minus_half[:],
                                   ALU.pow).then_inc(rstd_done[ln], 1)

            def chunk_c(c, has_next):
                for hc in range(HC):
                    if hc == 2 and has_next:
                        inverse_deviation(0, ln1_step, c + 1)
                    pool.wait_ge(h_hi_done, HC * c + hc + 1)
                    pool.tensor_tensor(h_lo[:, hc, :], h_sb[hc % 3][:], h_hi[:, hc, :],
                                       ALU.subtract).then_inc(h_lo_done, 1)
                inverse_deviation(1, ln2_step, c)

            inverse_deviation(0, ln1_step, 0)
            with pool.Fori(0, NCH - 1) as c:
                chunk_c(c, True)
            chunk_c(NCH - 1, False)

        @block.scalar
        def _(act):
            for u in range(0, len(units), 2):
                act.wait_ge(wt_ready, u + 1)
                act.copy(units[u][2], unit_bank(u)).then_inc(wt_copied[0], 1)

            act.sem_inc(xt_copied[0], 1)
            act.sem_inc(part1_done, 2)
            act.sem_inc(v_copied[0], 1)
            for m in range(4):
                act.sem_inc(parts_stored[m], 16)

            def copy_xt(c, par):
                act.wait_ge(xt_ready, 2 * c + 1)
                act.wait_ge(v_ready, 2 * c + 2)
                act.copy(x_t[par][:, 0, :], ps[:, 0, :]).then_inc(xt_copied[0], 1)

            def part0(c, m):
                act.wait_ge(qk_ready, 4 * c + m + 1)
                act.wait_ge(parts_stored[m], 16 * c + 16)
                act.copy(parts[m][:, 0, :], ps[:, 2 + m, :]).then_inc(part0_done, 1)

            def part1(c, m):
                act.wait_ge(qk_bank_free, 4 * c + 4 + m + 1)
                act.copy(parts[m][:, 1, :], rest[m % 2][:]).then_inc(part1_done, 1)

            def chunk_a(c, i, par, has_next):
                if has_next:
                    copy_xt(c + 1, 1 - par)
                part0(c, 0)
                part0(c, 1)
                part1(c, 0)
                part0(c, 2)
                part1(c, 1)
                part0(c, 3)
                part1(c, 2)
                part1(c, 3)
                act.wait_ge(v_ready, 2 * c + 4 + 1)
                act.wait_ge(v_stored[par], 16 * i + 16)
                act.copy(v_sb[par][:, 0:2, :].rearrange("p t d -> p (t d)"), ps[:, 6, :]).then_inc(v_copied[0], 1)

            copy_xt(0, 0)
            with act.Fori(0, PAIRS_LOOPED) as i:
                for par in range(2):
                    chunk_a(2 * i + par, i, par, True)
            for par in range(2):
                chunk_a(2 * PAIRS_LOOPED + par, PAIRS_LOOPED, par, par == 0)

            act.sem_inc(exp_done, 2)
            act.sem_inc(o_copied, 1)

            def copy_max_rows(turned):
                act.wait_ge(max_turned, turned)
                act.copy(max_rows[:, :], bank_bf(7)[0:3 * NM, 0:P]).then_inc(turn_free, 1)

            copy_max_rows(1)

            def exponential(n, st, pv):
                s, j = divmod(n, HG)
                w = slots[s % NS][2] * P
                act.wait_ge(st_ready, st + 1)
                if j == 0:
                    act.wait_ge(pv_done, pv)
                act.activation(probs[s % 3][:, j, 0:w], ps[:, 4 + n % 2, 0:w], ACT.Exp,
                               scale=SOFT_SCALE).then_inc(exp_done, 1)

            for n in range(HG * AHEAD):
                exponential(n, n, n // HG + 1)

            def group_b(b, g, b_last):
                def copy_o(half):
                    act.wait_ge(pv_done, at(b, g, NS, 3 + HALF_END[half] + 1))
                    act.wait_ge(o_turned, at(b, g, 2, 1 + half))
                    act.copy(o_sb[:], ps[:, 6, :]).then_inc(o_copied, 1)

                for step in group_steps(b_last, g):
                    if step[0] == "st":
                        _, s, j = step
                        exponential(HG * s + j, at(b, g, NE, HG * s + j), at(b, g, NS, s + 1))
                    elif step[0] == "oC":
                        copy_o(step[1])
                    elif step[0] == "mT":
                        act.wait_ge(max_rows_loaded, at(b, g, 48, 48))
                        copy_max_rows(at(b, g, 1, 2))

            with act.Fori(0, B - 1) as b:
                for g in range(NG):
                    group_b(b, g, False)
            for g in range(NG):
                group_b(B - 1, g, True)

            def copy_at(c):
                act.wait_ge(at_ready, 2 * c + 1)
                act.wait_ge(proj_ready, 2 * c + 2)
                act.copy(a_t[:, 0, :], ps[:, 0, :]).then_inc(at_copied[0], 1)

            def x1_high(c):
                for kc in range(KC):
                    act.wait_ge(x1t_ready, 2 * c + kc + 1)
                    act.copy(x1_hi[:, kc, :], ps[:, kc, :]).then_inc(x1_hi_done, 1)

            def chunk_c(c, par, has_next):
                if has_next:
                    copy_at(c + 1)
                for hc in range(HC + 1):
                    if hc < HC:
                        act.wait_ge(gate_ready, HC * c + hc + 1)
                        act.wait_ge(h_done, HC * c + hc + 1)
                        act.activation(silu[hc % 2][:], ps[:, 4 + 2 * (hc % 2), :], ACT.Silu,
                                       scale=W_SCALE).then_inc(silu_done, 1)
                    if hc >= 1:
                        if hc == 1:
                            act.wait_ge(down_ready, 2 * c + 2)
                        act.wait_ge(h_done, HC * c + 2 + hc)
                        act.copy(h_hi[:, hc - 1, :], h_sb[(hc - 1) % 3][:]).then_inc(h_hi_done, 1)
                if has_next:
                    x1_high(c + 1)

            copy_at(0)
            x1_high(0)
            with act.Fori(0, PAIRS_LOOPED) as i:
                for par in range(2):
                    chunk_c(2 * i + par, par, True)
            for par in range(2):
                chunk_c(2 * PAIRS_LOOPED + par, par, par == 0)

        @block.vector
        def _(dve):
            for name, n_, b_ in (("gate", wgate_n, wgate_b), ("up", wup_n, wup_b), ("down", wdown_n, wdown_b)):
                dve.wait_ge(w_loaded[name], 16)
                dve.tensor_copy(b_[:], n_[:]).then_inc(w_cast, 1)
            for u in range(1, len(units), 2):
                dve.wait_ge(wt_ready, u + 1)
                dve.tensor_copy(units[u][2], unit_bank(u)).then_inc(wt_copied[1], 1)

            dve.sem_inc(xt_copied[1], 1)
            dve.sem_inc(qk_bank_free, 4)
            dve.sem_inc(part2_done, 2)
            dve.sem_inc(v_copied[1], 1)
            for par in range(2):
                dve.sem_inc(v_stored[par], 16)

            def copy_xt(c, par):
                dve.wait_ge(xt_ready, 2 * c + 2)
                dve.wait_ge(v_ready, 2 * c + 2)
                dve.tensor_copy(x_t[par][:, 1, :], ps[:, 1, :]).then_inc(xt_copied[1], 1)

            def rest_of(c, m):
                dve.wait_ge(part0_done, 4 * c + m + 1)
                dve.wait_ge(part1_done, 4 * c + m + 1)
                dve.wait_ge(part2_done, 4 * c + m + 1)
                dve.tensor_tensor(rest[m % 2][:], ps[:, 2 + m, :], parts[m][:, 0, :],
                                  ALU.subtract).then_inc(qk_bank_free, 1)

            def part2(c, m):
                dve.wait_ge(part1_done, 4 * c + 2 + m + 1)
                dve.tensor_tensor(parts[m][:, 2, :], rest[m % 2][:], parts[m][:, 1, :],
                                  ALU.subtract).then_inc(part2_done, 1)

            def chunk_a(c, i, par, has_next):
                if has_next:
                    copy_xt(c + 1, 1 - par)
                rest_of(c, 0)
                rest_of(c, 1)
                part2(c, 0)
                rest_of(c, 2)
                part2(c, 1)
                rest_of(c, 3)
                part2(c, 2)
                part2(c, 3)
                dve.wait_ge(v_ready, 2 * c + 4 + 2)
                dve.wait_ge(v_stored[par], 16 * i + 16)
                dve.tensor_copy(v_sb[par][:, 2:4, :].rearrange("p t d -> p (t d)"),
                                ps[:, 7, :]).then_inc(v_copied[1], 1)

            copy_xt(0, 0)
            with dve.Fori(0, PAIRS_LOOPED) as i:
                for par in range(2):
                    chunk_a(2 * i + par, i, par, True)
            for par in range(2):
                chunk_a(2 * PAIRS_LOOPED + par, PAIRS_LOOPED, par, par == 0)

            dve.sem_inc(s_free, 2)
            dve.sem_inc(turn_free, 1)
            for half in range(2):
                dve.sem_inc(attn_stored[half], 16)
            dve.wait_ge(consts_ready, 5)

            def row_maximum(n, m):
                w = max_items[m] * P
                dve.wait_ge(s_ready, n + 1)
                dve.sem_inc(dve_passed, 1)
                scores = ps[:, 2 * (m % 2):2 * (m % 2) + 2, :].rearrange("p a b -> p (a b)")[:, 0:w]
                dve.tensor_tensor_reduce(scores, scores, causal[:, T - w:T], 1.0, LOWEST, ALU.add, ALU.max,
                                         row_max[:, m:m + 1]).then_inc(s_free, 1)

            def split_max(count, maxima, k):
                a = dve
                a.wait_ge(s_free, 2 + maxima)
                if k:
                    a.wait_ge(max_turned, count)
                a.tensor_copy(max_parts[:, 0, :], row_max[:]).then_inc(max_step, 1)
                a.wait_ge(max_step, 4 * count + 1)
                a.tensor_tensor(max_rest[:, 0, :], row_max[:], max_parts[:, 0, :], ALU.subtract).then_inc(max_step, 1)
                a.wait_ge(max_step, 4 * count + 2)
                a.tensor_copy(max_parts[:, 1, :], max_rest[:, 0, :]).then_inc(max_step, 1)
                a.wait_ge(max_step, 4 * count + 3)
                a.tensor_tensor(max_rest[:, 1, :], max_rest[:, 0, :], max_parts[:, 1, :], ALU.subtract).then_inc(max_step, 1)
                a.wait_ge(max_step, 4 * count + 4)
                a.tensor_copy(max_parts[:, 2, :], max_rest[:, 1, :]).then_inc(max_parts_ready, 1)

            for k in range(2):
                for m in range(NM):
                    row_maximum(NM * k + m, m)
                split_max(k, NM * (k + 1), k)

            def group_b(b, g, b_last):
                def normalise(half):
                    turned = ps[:, 7, :].rearrange("p (t j e) -> p t j e", t=HQ, j=HG)
                    dve.wait_ge(o_turned, at(b, g, 2, 1 + half + 1))
                    dve.reciprocal(recip[:], turned[:, :, :, DH]).then_inc(recip_done, 1)
                    dve.wait_ge(recip_done, at(b, g, 2, half + 1))
                    dve.wait_ge(attn_stored[half], at(b, g, 16, 16))
                    dve.tensor_tensor(attn_sb[half][:], turned[:, :, :, 0:DH],
                                      recip[:].unsqueeze(3).to_broadcast([P, HQ, HG, DH]),
                                      ALU.mult).then_inc(turn_free, 1)

                steps = group_steps(b_last, g)
                for step in steps:
                    if step[0] == "max":
                        m = step[1]
                        row_maximum(at(b, g, NM, 2 * NM + m), m)
                        if m == NM - 1:
                            split_max(at(b, g, 1, 2), at(b, g, NM, 3 * NM), 1)
                    elif step[0] == "oT":
                        normalise(step[1])

            with dve.Fori(0, B - 1) as b:
                for g in range(NG):
                    group_b(b, g, False)
            for g in range(NG):
                group_b(B - 1, g, True)

            dve.sem_inc(x1_lo_done, 2)
            dve.sem_inc(h_done, 2)
            dve.sem_inc(z_done, 2)
            for par in range(2):
                dve.sem_inc(out_stored[par], 16)

            def copy_at(c):
                dve.wait_ge(at_ready, 2 * c + 2)
                dve.wait_ge(proj_ready, 2 * c + 2)
                dve.tensor_copy(a_t[:, 1, :], ps[:, 1, :]).then_inc(at_copied[1], 1)

            def y_bank(c, i, par, k):
                if k == 0:
                    dve.wait_ge(xa_loaded[par], 32 * i + 32)
                dve.wait_ge(proj_ready, 2 * c + 2 + k + 1)
                dve.tensor_tensor(x1[par][:, 2 * k:2 * k + 2, :].rearrange("p t d -> p (t d)"), ps[:, 2 + k, :],
                                  x_sb[par][:, 2 * k:2 * k + 2, :].rearrange("p t d -> p (t d)"),
                                  ALU.add).then_inc(y_done, 1)

            def ln_stats(ln, step, c, buf, tiles):
                for t in tiles:
                    last = dve.bn_stats(stats[:, ln, t, :], buf[:, t, :])
                if TILES - 1 in tiles:
                    last.then_inc(step, 1)

            def ln_variance(ln, step, c):
                dve.wait_ge(step, 3 * c + 1)
                dve.sem_inc(dve_passed, 1)
                for t in range(TILES):
                    last = dve.bn_aggr(mean_var[:, ln, t, :], stats[:, ln, t, :])
                last.then_inc(step, 1)
                dve.wait_ge(step, 3 * c + 2)
                dve.tensor_scalar(var_eps[:, ln, :], mean_var[:, ln, :, 1], EPS, None, ALU.add).then_inc(step, 1)

            def ln_apply(ln, c, buf, done):
                dve.wait_ge(rstd_done[ln], c + 1)
                for t in range(TILES):
                    last = dve.tensor_scalar(buf[:, t, :], buf[:, t, :], mean_var[:, ln, t, 0:1],
                                             rstd[:, ln, t:t + 1], ALU.subtract, ALU.mult)
                last.then_inc(done, 1)

            def x1_low(c):
                for kc in range(KC):
                    dve.wait_ge(x1_hi_done, 2 * c + kc + 1)
                    dve.tensor_tensor(x1_lo[:, kc, :], ps[:, kc, :], x1_hi[:, kc, :],
                                      ALU.subtract).then_inc(x1_lo_done, 1)

            def hidden(c, hc):
                dve.wait_ge(silu_done, HC * c + hc + 1)
                dve.wait_ge(up_ready, HC * c + hc + 1)
                dve.wait_ge(h_lo_done, HC * c + hc + 1)
                dve.scalar_tensor_tensor(out=h_sb[hc % 3][:], in0=ps[:, 5 + 2 * (hc % 2), :], scalar=0.5 * W_SCALE,
                                         in1=silu[hc % 2][:], op0=ALU.mult, op1=ALU.mult).then_inc(h_done, 1)

            def chunk_c(c, i, par, has_next):
                n, ni, npar = c + 1, i + par, 1 - par
                if has_next:
                    copy_at(n)
                    y_bank(n, ni, npar, 0)
                    y_bank(n, ni, npar, 1)
                hidden(c, 0)
                if has_next:
                    dve.wait_ge(y_done, 2 * n + 2)
                    ln_stats(0, ln1_step, n, x1[npar], (0, 1))
                hidden(c, 1)
                if has_next:
                    ln_stats(0, ln1_step, n, x1[npar], (2, 3))
                    ln_variance(0, ln1_step, n)
                hidden(c, 2)
                hidden(c, 3)
                if has_next:
                    ln_apply(0, n, x1[npar], x1_ready)
                hidden(c, 4)
                hidden(c, 5)
                if has_next:
                    x1_low(n)
                for k in range(2):
                    dve.wait_ge(down_ready, 2 * c + 2 + k + 1)
                    if k == 0:
                        dve.wait_ge(out_stored[par], 16 * i + 16)
                    dve.scalar_tensor_tensor(out=z_sb[par][:, 2 * k:2 * k + 2, :].rearrange("p t d -> p (t d)"),
                                             in0=ps[:, 2 + k, :], scalar=2.0 * W_SCALE,
                                             in1=x1[par][:, 2 * k:2 * k + 2, :].rearrange("p t d -> p (t d)"),
                                             op0=ALU.mult, op1=ALU.add).then_inc(z_done, 1)
                dve.wait_ge(z_done, 2 * c + 4)
                ln_stats(1, ln2_step, c, z_sb[par], range(TILES))
                ln_variance(1, ln2_step, c)
                ln_apply(1, c, z_sb[par], out_ready)

            copy_at(0)
            y_bank(0, 0, 0, 0)
            y_bank(0, 0, 0, 1)
            dve.wait_ge(y_done, 2)
            ln_stats(0, ln1_step, 0, x1[0], range(TILES))
            ln_variance(0, ln1_step, 0)
            ln_apply(0, 0, x1[0], x1_ready)
            x1_low(0)
            with dve.Fori(0, PAIRS_LOOPED) as i:
                for par in range(2):
                    chunk_c(2 * i + par, i, par, True)
            for par in range(2):
                chunk_c(2 * PAIRS_LOOPED + par, PAIRS_LOOPED, par, par == 0)

        @block.tensor
        def _(pe):
            pe.wait_ge(consts_ready, 5)
            for u, (name, tiles, dst) in enumerate(units):
                pe.wait_ge(w_loaded[name], 16)
                if name in casts:
                    pe.wait_ge(w_cast, casts[name])
                if u >= 8:
                    pe.wait_ge(wt_copied[u % 2], (u - 8) // 2 + 1)
                bank = unit_bank(u)
                for n, tile in enumerate(tiles):
                    last = pe.transpose(bank[:, tile_cols(n)], tile, ident_bf[:] if name in casts else ident[:])
                last.then_inc(wt_ready, 1)
            pe.wait_ge(wt_copied[0], (len(units) + 1) // 2)
            pe.wait_ge(wt_copied[1], len(units) // 2)

            pe.sem_inc(v_ready, 4)

            def turn_x(c, i, par):
                pe.wait_ge(x_loaded[par], 16 * i + 16)
                for kc in range(KC):
                    pe.wait_ge(xt_copied[kc], c + 1)
                    for t in range(TILES):
                        last = pe.transpose(ps[:, kc, tile_cols(t)], x_sb[par][:, t, kc * P:(kc + 1) * P], ident[:])
                    last.then_inc(xt_ready, 1)

            def chunk_a(c, i, par, has_next):
                if has_next:
                    turn_x(c + 1, i + par, 1 - par)
                pe.wait_ge(xt_copied[0], c + 2)
                pe.wait_ge(xt_copied[1], c + 2)
                for m in range(4):
                    pe.wait_ge(qk_bank_free, 4 * c + m + 1)
                    for kc in range(KC):
                        last = pe.matmul(ps[:, 2 + m, :], wqkv_t[:, kc, m * P:(m + 1) * P], x_t[par][:, kc, :],
                                         start=kc == 0, stop=kc == KC - 1)
                    last.then_inc(qk_ready, 1)
                for k in range(2):
                    pe.wait_ge(v_copied[k], c + 1)
                    for t in (2 * k, 2 * k + 1):
                        for kc in range(KC):
                            last = pe.matmul(ps[:, 6 + k, (t % 2) * D:(t % 2 + 1) * D], x_t[par][:, kc, tile_cols(t)],
                                             wqkv_t[:, kc, 2 * D:3 * D], start=kc == 0, stop=kc == KC - 1)
                    last.then_inc(v_ready, 1)

            turn_x(0, 0, 0)
            with pe.Fori(0, PAIRS_LOOPED) as i:
                for par in range(2):
                    chunk_a(2 * i + par, i, par, True)
            for par in range(2):
                chunk_a(2 * PAIRS_LOOPED + par, PAIRS_LOOPED, par, par == 0)
            for k in range(2):
                pe.wait_ge(xt_copied[k], NCH + 1)
                pe.wait_ge(v_copied[k], NCH + 1)
            pe.wait_ge(qk_bank_free, 4 * NCH + 4)

            pe.wait_ge(preset, 6)

            pe.sem_inc(pv_done, 3)
            pe.sem_inc(o_turned, 1)

            def scores_for_max(g, n, m):
                j, qt = m // QT, m % QT
                pe.wait_ge(s_free, n + 1)
                for k0 in range(0, (qt + 1) * P, CH):
                    w = min(CH, (qt + 1) * P - k0)
                    last = pe.matmul(ps[:, 2 * (m % 2) + k0 // CH, 0:w], q_stack[g][0:ROWS, j, tile_cols(qt)],
                                     k_stack[g][0:ROWS, j, k0:k0 + w], start=True, stop=True)
                last.then_inc(s_ready, 1)

            def turn_max(ready, bank_use):
                pe.wait_ge(max_parts_ready, ready)
                pe.wait_ge(turn_free, bank_use + 1)
                pe.transpose(bank_bf(7)[0:3 * NM, 0:P], max_parts[:].rearrange("p a b -> p (a b)"),
                             ident_bf[:]).then_inc(max_turned, 1)

            for k in range(2):
                pe.wait_ge(stack_loaded[k], 16 * 12)
                for m in range(NM):
                    scores_for_max(k, NM * k + m, m)
                    if k == 1 and m == 1:
                        turn_max(1, 0)

            def scores(g, n, st):
                s, j = divmod(n, HG)
                half, kt, w = slots[s]
                q0 = max(half * HQ, kt) * P
                pe.wait_ge(exp_done, st + 1)
                pe.matmul(ps[:, 4 + n % 2, 0:w * P], k_stack[g][0:ROWS_M, j, tile_cols(kt)],
                          q_stack[g][0:ROWS_M, j, q0:q0 + w * P], start=True, stop=True).then_inc(st_ready, 1)

            pe.wait_ge(max_rows_loaded, 48)
            for n in range(HG * AHEAD):
                scores(0, n, n)

            def group_b(b, g, b_last):
                for step in group_steps(b_last, g):
                    if step[0] == "st":
                        _, s, j = step
                        if s == NS and j == 0:
                            pe.wait_ge(max_rows_loaded, at(b, g, 48, 96))
                        scores((g + s // NS) % NG, HG * (s % NS) + j, at(b, g, NE, HG * s + j))
                    elif step[0] == "pv":
                        s = step[1]
                        half, kt, w = slots[s]
                        c0 = (max(half * HQ, kt) - half * HQ) * P
                        if s == 0:
                            pe.wait_ge(v_expanded, at(b, g, 1, 1))
                        if kt == 0:
                            pe.wait_ge(o_copied, at(b, g, 2, 1 + half))
                        if s in diagonal:
                            pe.wait_ge(masked, at(b, g, ND, diagonal.index(s) + 1))
                        else:
                            pe.wait_ge(exp_done, at(b, g, NE, 2 + HG * (s + 1)))
                        for j in range(HG):
                            last = pe.matmul(ps[32 * j:32 * j + 32, 6, c0:c0 + w * P], v_ones[g % 2][:, kt, j, :],
                                             probs[s % 3][:, j, 0:w * P], start=kt == 0, stop=s == HALF_END[half])
                        last.then_inc(pv_done, 1)
                    elif step[0] == "max":
                        m = step[1]
                        if m == 0:
                            pe.wait_ge(stack_loaded[(g + 2) % NG], 192 * (b + (g + 2) // NG + 1))
                        scores_for_max((g + 2) % NG, at(b, g, NM, 2 * NM + m), m)
                    elif step[0] == "mT":
                        turn_max(at(b, g, 1, 2), turn_use(b, g, b_last, 0))
                    elif step[0] == "oT":
                        half = step[1]
                        pe.wait_ge(o_copied, at(b, g, 2, 1 + half + 1))
                        pe.wait_ge(turn_free, turn_use(b, g, b_last, 1 + half) + 1)
                        for t in range(HQ):
                            last = pe.transpose(ps[:, 7, tile_cols(t)], o_sb[:, tile_cols(t)], ident[:])
                        last.then_inc(o_turned, 1)

            with pe.Fori(0, B - 1) as b:
                for g in range(NG):
                    group_b(b, g, False)
            for g in range(NG):
                group_b(B - 1, g, True)
            pe.wait_ge(s_free, 2 + NM * GROUPS)
            pe.wait_ge(exp_done, 2 + NE * GROUPS)
            pe.wait_ge(o_copied, 1 + 2 * GROUPS)
            pe.wait_ge(turn_free, 1 + 3 * GROUPS)

            pe.sem_inc(proj_ready, 2)
            pe.sem_inc(down_ready, 2)

            def turn_attn(c, i, par):
                pe.wait_ge(xa_loaded[par], 32 * i + 32)
                pe.wait_ge(x1_lo_done, 2 * c + 2)
                for kc in range(KC):
                    for t in range(TILES):
                        last = pe.transpose(ps[:, kc, tile_cols(t)], a_sb[par][:, t, kc * P:(kc + 1) * P], ident[:])
                    last.then_inc(at_ready, 1)

            def project(c):
                pe.wait_ge(at_copied[0], c + 1)
                pe.wait_ge(at_copied[1], c + 1)
                for t in range(TILES):
                    for kc in range(KC):
                        last = pe.matmul(ps[:, 2 + t // 2, (t % 2) * D:(t % 2 + 1) * D], a_t[:, kc, tile_cols(t)],
                                         wproj_t[:, kc, :], start=kc == 0, stop=kc == KC - 1)
                    if t % 2:
                        last.then_inc(proj_ready, 1)

            def turn_x1(c, par):
                pe.wait_ge(x1_ready, c + 1)
                for kc in range(KC):
                    for t in range(TILES):
                        last = pe.transpose(ps[:, kc, tile_cols(t)], x1[par][:, t, kc * P:(kc + 1) * P], ident[:])
                    last.then_inc(x1t_ready, 1)

            def chunk_c(c, i, par, has_next):
                if has_next:
                    turn_attn(c + 1, i + par, 1 - par)
                    pe.wait_ge(z_done, 2 * c + 2)
                    project(c + 1)
                pe.wait_ge(x1_lo_done, 2 * c + 4)
                for hc in range(HC):
                    pe.wait_ge(h_done, HC * c + hc + 1)
                    for w, bank, ready in ((wgate_t, 4, gate_ready), (wup_t, 5, up_ready)):
                        for kc in range(KC):
                            for part in (x1_hi, x1_lo):
                                last = pe.matmul(ps[:, bank + 2 * (hc % 2), :], w[:, kc, hc * P:(hc + 1) * P], part[:, kc, :],
                                                 start=kc == 0 and part is x1_hi, stop=kc == KC - 1 and part is x1_lo)
                        last.then_inc(ready, 1)
                if has_next:
                    turn_x1(c + 1, 1 - par)
                    pe.wait_ge(y_done, 2 * c + 4)
                pe.wait_ge(h_lo_done, HC * c + 3 + HC)
                for t in range(TILES):
                    for hc in range(HC):
                        for part in (h_hi, h_lo):
                            last = pe.matmul(ps[:, 2 + t // 2, (t % 2) * D:(t % 2 + 1) * D], part[:, hc, tile_cols(t)],
                                             wdown_t[:, hc, :], start=hc == 0 and part is h_hi,
                                             stop=hc == HC - 1 and part is h_lo)
                    if t % 2:
                        last.then_inc(down_ready, 1)

            turn_attn(0, 0, 0)
            project(0)
            turn_x1(0, 0)
            with pe.Fori(0, PAIRS_LOOPED) as i:
                for par in range(2):
                    chunk_c(2 * i + par, i, par, True)
            for par in range(2):
                chunk_c(2 * PAIRS_LOOPED + par, PAIRS_LOOPED, par, par == 0)


_INS = ["L0_attn_x", "L0_attn_W_qkv", "L0_attn_W_proj", "L0_ffn_w_gate", "L0_ffn_w_up", "L0_ffn_w_down"]


def kernel(**inputs):
    import numpy as _np
    import concourse.bacc as _bacc
    from concourse import mybir as _mybir
    from concourse.bass_utils import run_bass_kernel_spmd as _run

    nc = _bacc.Bacc("TRN2", target_bir_lowering=False, num_devices=1)
    arrays, args = {}, []
    for name in _INS:
        a = _np.ascontiguousarray(inputs[name])
        arrays[f"in_{name}"] = a
        args.append(nc.dram_tensor(f"in_{name}", a.shape, _mybir.dt.from_np(a.dtype), kind="ExternalInput").ap())
    out = nc.dram_tensor("out_x", inputs["L0_attn_x"].shape, F32, kind="ExternalOutput").ap()
    block_kernel(nc, *args, out)
    r = _run(nc, [arrays], core_ids=[0])
    return r.results[0]["out_x"]
```

```python
from contextlib import ExitStack

import concourse.bass as bass
from concourse import mybir

F32 = mybir.dt.float32
BF16 = mybir.dt.bfloat16
F16 = mybir.dt.float16
I32 = mybir.dt.int32
ALU = mybir.AluOpType
ACT = mybir.ActivationFunctionType


RING = 3


def attention_steps(slots, diagonal, unit_items, ahead, has_max, has_m, has_st):
    COLS, EXP, ROW_MAX, PV, TURN = 54, (50, 107), (68, 134), (80, 214), 428
    MASK, COPY, COPY_ROWS, NORMALISE, SPLIT = 594, 478, 158, 650, 950
    PE_ACT, PE_DVE, ACT_PE, DVE_PE, ACT_POOL, POOL_PE = 200, 270, 110, 170, 230, 180
    LEAD_ST = 0.05
    ns, nu, hg = len(slots), len(unit_items), 4
    whole = hg * sum(w for _, _, w in slots)
    pe = act = dve = pool = o_free = 0
    st_free, s_free = [0, 0, 0], [0, 0]
    pv_ready, pairs_used = {s: 0 for s in range(ahead)}, 0
    for turn in range(4):
        n, end, m, p = hg * ahead, hg * (ns + ahead * has_st), 0, 0
        st_cols = max_cols = pv_cols = 0
        turns, order, pv_end, next_ready = [], [], {}, {}
        while n < end or p < ns or turns or (has_max and m < nu):
            could = []
            if n < end and n // hg < p + RING:
                could.append((st_free[n % 3], st_cols / whole - LEAD_ST, "st"))
            if has_max and m < nu:
                could.append((s_free[pairs_used % 2], max_cols / whole, "max"))
            if p < ns and p in pv_ready:
                could.append((max(pv_ready[p], o_free if slots[p][1] == 0 else 0), pv_cols / whole, "pv"))
            if turns:
                could.append((max(turns[0][1], s_free[pairs_used % 2]), -1, "oT"))
            ready = [c for c in could if c[0] <= pe] or [min(could)]
            start, _, what = min(ready, key=lambda c: c[1])
            pe = max(pe, start)
            if what == "st":
                s, j = divmod(n, hg)
                w = slots[s % ns][2]
                order.append(("st", s, j))
                pe += max(w * COLS, 90)
                room = pv_end.get(s - RING, 0) + PE_ACT if j == 0 else 0
                act = max(act, pe + PE_ACT, room) + EXP[0] + w * EXP[1]
                st_free[n % 3] = act + ACT_PE
                n, st_cols = n + 1, st_cols + w
                if j == hg - 1:
                    ready_at = act + ACT_PE
                    if s % ns in diagonal:
                        pool = max(pool, act + ACT_POOL) + MASK
                        ready_at = pool + POOL_PE
                    (pv_ready if s < ns else next_ready)[s % ns] = ready_at
                if n == hg * (ahead + 1) and has_m:
                    order.append(("mT",))
                    pe = max(pe, st_free[0]) + COLS
                    act = max(act, pe + PE_ACT) + COPY_ROWS
                    st_free[0] = act + ACT_PE
            elif what == "max":
                order.append(("max", m))
                cols = sum(qt + 1 for _, qt in unit_items[m])
                pe += cols * COLS
                dve = max(dve, pe + PE_DVE) + len(unit_items[m]) * ROW_MAX[0] + cols * ROW_MAX[1]
                s_free[pairs_used % 2] = dve + DVE_PE
                m, max_cols, pairs_used = m + 1, max_cols + cols, pairs_used + 1
                if m == nu:
                    dve += SPLIT
            elif what == "pv":
                order.append(("pv", p))
                pe += PV[0] + slots[p][2] * PV[1]
                pv_end[p] = pe
                p, pv_cols = p + 1, pv_cols + hg * slots[p][2]
                if p == ns or slots[p][0] != slots[p - 1][0]:
                    half = slots[p - 1][0]
                    order.append(("oC", half))
                    act = max(act, pe + PE_ACT) + COPY
                    o_free = act + ACT_PE
                    turns.append((half, o_free))
            else:
                order.append(("oT", turns.pop(0)[0]))
                pe += TURN
                dve = max(dve, pe + PE_DVE) + NORMALISE
                s_free[pairs_used % 2] = dve + DVE_PE
                pairs_used += 1
        pv_ready = next_ready
        if not (has_st and has_max):
            break
    return order


def block_kernel(nc, x, w_qkv, w_proj, w_gate, w_up, w_down, out):
    P = 128
    B, T, D = x.shape
    HID = w_gate.shape[0]
    H = 16
    DH = D // H
    NTOK = B * T
    CH = 512
    NCH = NTOK // CH
    TILES = CH // P
    KC = D // P
    HC = HID // P
    QT = T // P
    HG = 4
    NG = H // HG
    GROUPS = B * NG
    EPS = 1e-5
    SOFT_SCALE = 1.0 / float(DH) ** 0.5
    W_SCALE = 1.0 / 127.0
    LOWEST = -3.0e38
    PAIRS = [(0, 0), (1, 0), (2, 0), (0, 1), (1, 1), (0, 2)]
    ROWS = len(PAIRS) * DH
    ROWS_M = ROWS + 3

    HQ = QT // 2
    slots = [(0, kt, HQ - kt) for kt in range(HQ)]
    slots += [(1, kt, min(HQ, QT - kt)) for kt in range(QT)]
    diagonal = [s for s, (half, kt, w) in enumerate(slots) if kt >= half * HQ]
    NS = len(slots)
    NE = NS * HG
    NM = HG * QT
    ND = len(diagonal)
    NR = NE + 1
    max_units = []
    for j in range(0, HG, 2):
        for k in (j, j + 1):
            max_units += [[(k, QT - 1)]] + [[(k, QT - 1 - t), (k, t - 1)] for t in range(1, QT // 2)]
        max_units.append([(j, QT // 2 - 1), (j + 1, QT // 2 - 1)])
    NU = len(max_units)
    NP = NU + 2
    HALF_END = [HQ - 1, NS - 1]
    AHEAD = 2

    xf = x.rearrange("b t d -> (b t) d")
    of = out.rearrange("b t d -> (b t) d")
    x_tiles = xf.rearrange("(c p) d -> p c d", p=P)
    out_tiles = of.rearrange("(c p) d -> p c d", p=P)
    qk_dram = nc.dram_tensor("qk_parts", [2, 3, D, NTOK], BF16, kind="Internal").ap()
    v_dram = nc.dram_tensor("v_rows", [NTOK, D], F32, kind="Internal").ap()
    a_dram = nc.dram_tensor("attn_rows", [NTOK, D], F32, kind="Internal").ap()
    v_tiles = v_dram.rearrange("(c p) d -> p c d", p=P)
    a_tiles = a_dram.rearrange("(c p) d -> p c d", p=P)

    with ExitStack() as ctx:
        def sb(name, shape, dt):
            return ctx.enter_context(nc.sbuf_tensor(name, shape, dt))

        def sem(name):
            return ctx.enter_context(nc.semaphore(name))

        ps = ctx.enter_context(nc.psum_tensor("ps", [P, 8, 512], F32))

        ident = sb("ident", [P, P], F32)
        ident_bf = sb("ident_bf", [P, P], BF16)
        causal = sb("causal", [P, T], F32)
        minus_half = sb("minus_half", [P, TILES], F32)
        wqkv_t = sb("wqkv_t", [P, KC, 3 * D], F32)
        wproj_t = sb("wproj_t", [P, KC, D], F32)
        wgate_t = sb("wgate_t", [P, KC, HID], BF16)
        wup_t = sb("wup_t", [P, KC, HID], BF16)
        wdown_t = sb("wdown_t", [P, HC, D], BF16)

        x_sb = [sb(f"x_sb{i}", [P, TILES, D], F32) for i in range(2)]
        x_t = [sb(f"x_t{i}", [P, KC, CH], F32) for i in range(2)]
        parts = [sb(f"parts{i}", [P, 3, CH], BF16) for i in range(4)]
        rest = [sb(f"rest{i}", [P, CH], F32) for i in range(2)]
        v_sb = [sb(f"v_sb{i}", [P, TILES, D], F32) for i in range(2)]
        with ExitStack() as early:
            def sb_early(name, shape, dt):
                return early.enter_context(nc.sbuf_tensor(name, shape, dt))

            wqkv_n = sb_early("wqkv_n", [P, 3 * KC, D], F32)
            wproj_n = sb_early("wproj_n", [P, KC, D], F32)
            wgate_n = sb_early("wgate_n", [P, HC, D], I32)
            wup_n = sb_early("wup_n", [P, HC, D], I32)
            wdown_n = sb_early("wdown_n", [P, KC, HID], I32)
            wgate_b = sb_early("wgate_b", [P, HC, D], BF16)
            wup_b = sb_early("wup_b", [P, HC, D], BF16)
            wdown_b = sb_early("wdown_b", [P, KC, HID], BF16)

        with ExitStack() as middle:
            def sb_middle(name, shape, dt):
                return middle.enter_context(nc.sbuf_tensor(name, shape, dt))

            q_stack = [sb_middle(f"q_stack{i}", [P, HG, T], BF16) for i in range(4)]
            v_flat = [sb_middle(f"v_flat{i}", [P, QT, HG * DH], F32) for i in range(2)]
            k_stack = [sb_middle(f"k_stack{i}", [P, HG, T], BF16) for i in range(4)]
            v_ones = [sb_middle(f"v_ones{i}", [P, QT, HG, 32], F32) for i in range(2)]
            probs = [sb_middle(f"probs{i}", [P, HG, CH], F32) for i in range(RING)]
            row_max = sb_middle("row_max", [P, NM], F32)
            max_rest = sb_middle("max_rest", [P, 2, NM], F32)
            max_parts = sb_middle("max_parts", [P, 3, NM], BF16)
            max_rows = sb_middle("max_rows", [3 * NM, P], BF16)
            o_sb = sb_middle("o_sb", [P, CH], F32)
            recip = sb_middle("recip", [P, 2, HQ, HG], F32)
            attn_sb = [sb_middle(f"attn_sb{i}", [P, HQ, HG, DH], F32) for i in range(2)]

        a_sb = v_sb
        a_t = x_t[0]
        x1 = [sb(f"x1_{i}", [P, TILES, D], F32) for i in range(2)]
        x1_hi = sb("x1_hi", [P, KC, CH], F16)
        x1_lo = sb("x1_lo", [P, KC, CH], F16)
        silu = [sb(f"silu{i}", [P, CH], F32) for i in range(2)]
        h_sb = [sb(f"h_sb{i}", [P, CH], F32) for i in range(3)]
        h_hi = sb("h_hi", [P, HC, CH], F16)
        h_lo = sb("h_lo", [P, HC, CH], F16)
        z_sb = [sb(f"z_sb{i}", [P, TILES, D], F32) for i in range(2)]
        stats = sb("stats", [P, 2, TILES, 6], F32)
        mean_var = sb("mean_var", [P, 2, TILES, 2], F32)
        var_eps = sb("var_eps", [P, 2, TILES], F32)
        rstd = sb("rstd", [P, 2, TILES], F32)

        w_loaded = {n: sem(f"w_loaded_{n}") for n in ("qkv", "proj", "gate", "up", "down")}
        consts_ready = sem("consts_ready")
        preset = sem("preset")
        w_cast = sem("w_cast")
        wt_ready = sem("wt_ready")
        wt_copied = [sem("wt_copied_act"), sem("wt_copied_dve")]
        dve_passed = sem("dve_passed")
        pool_passed = sem("pool_passed")
        sp_passed = sem("sp_passed")
        x_loaded = [sem(f"x_loaded{i}") for i in range(2)]
        xt_ready = sem("xt_ready")
        xt_copied = [sem("xt_copied_act"), sem("xt_copied_dve")]
        qk_ready = sem("qk_ready")
        part0_done = sem("part0_done")
        qk_bank_free = sem("qk_bank_free")
        part1_done = sem("part1_done")
        part2_done = sem("part2_done")
        parts_stored = [sem(f"parts_stored{i}") for i in range(4)]
        v_ready = sem("v_ready")
        v_copied = [sem("v_copied_act"), sem("v_copied_dve")]
        v_stored = [sem(f"v_stored{i}") for i in range(2)]
        stack_loaded = [sem(f"stack_loaded{i}") for i in range(4)]
        v_loaded = [sem(f"v_loaded{i}") for i in range(2)]
        v_expanded = sem("v_expanded")
        s_ready = sem("s_ready")
        s_free = sem("s_free")
        max_step = sem("max_step")
        max_parts_ready = sem("max_parts_ready")
        max_turned = sem("max_turned")
        max_rows_loaded = sem("max_rows_loaded")
        st_ready = sem("st_ready")
        exp_done = sem("exp_done")
        masked = sem("masked")
        pv_done = sem("pv_done")
        o_copied = sem("o_copied")
        recip_done = sem("recip_done")
        attn_stored = [sem(f"attn_stored{i}") for i in range(2)]
        xa_loaded = [sem(f"xa_loaded{i}") for i in range(2)]
        at_ready = sem("at_ready")
        at_copied = [sem("at_copied_act"), sem("at_copied_dve")]
        proj_ready = sem("proj_ready")
        y_done = sem("y_done")
        ln1_step = sem("ln1_step")
        rstd_done = [sem("rstd1_done"), sem("rstd2_done")]
        x1_ready = sem("x1_ready")
        x1t_ready = sem("x1t_ready")
        x1_hi_done = sem("x1_hi_done")
        x1_lo_done = sem("x1_lo_done")
        gate_ready = sem("gate_ready")
        up_ready = sem("up_ready")
        silu_done = sem("silu_done")
        h_done = sem("h_done")
        h_hi_done = sem("h_hi_done")
        h_lo_done = sem("h_lo_done")
        down_ready = sem("down_ready")
        z_done = sem("z_done")
        ln2_step = sem("ln2_step")
        out_ready = sem("out_ready")
        out_stored = [sem(f"out_stored{i}") for i in range(2)]

        def bank_bf(b):
            return ps[:, b, :].bitcast(BF16)

        units = []
        for kc in range(KC):
            for r in (0, 3):
                units.append(("qkv", [wqkv_n[:, r + i, kc * P:(kc + 1) * P] for i in range(3)],
                              wqkv_t[:, kc, r * P:(r + 3) * P]))
        for kc in range(KC):
            units.append(("proj", [wproj_n[:, r, kc * P:(kc + 1) * P] for r in range(KC)], wproj_t[:, kc, :]))
        for name, src, dst in (("gate", wgate_b, wgate_t), ("up", wup_b, wup_t)):
            for kc in range(KC):
                for r in (0, 3):
                    units.append((name, [src[:, r + i, kc * P:(kc + 1) * P] for i in range(3)],
                                  dst[:, kc, r * P:(r + 3) * P]))
        for hc in range(0, HC, 2):
            units.append(("down", [wdown_b[:, r, (hc + i) * P:(hc + i + 1) * P] for i in range(2) for r in range(KC)],
                          wdown_t[:, hc:hc + 2, :].rearrange("p a b -> p (a b)")))
        casts = {"gate": 1, "up": 2, "down": 3}

        def unit_bank(u):
            name, tiles, dst = units[u]
            bank = bank_bf(u % 8) if name in casts else ps[:, u % 8, :]
            return bank[:, 0:len(tiles) * P]

        PAIRS_LOOPED = NCH // 2 - 1
        PAIRS_C = NCH // 2 - 2

        def tile_cols(t):
            return slice(t * P, (t + 1) * P)

        def group_steps(b_last, g):
            return attention_steps(slots, diagonal, max_units, AHEAD, not (b_last and g >= NG - 2),
                                   not (b_last and g == NG - 1), not (b_last and g == NG - 1))

        def at(b, g, per, n):
            return b * (NG * per) + (g * per + n)

        def bank_use(b, g, b_last, n):
            behind_maxima = n >= HG * (AHEAD + 1) and not (b_last and g == NG - 1)
            return at(b, g, NR, 1 + n + (1 if behind_maxima else 0))

        def maxima_use(b, g):
            return at(b, g, NR, 1 + HG * (AHEAD + 1))

        def pair_use(b, g, b_last, step):
            k = [s for s in group_steps(b_last, g) if s[0] in ("max", "oT")].index(step)
            return at(b, g, NP, 2 * NU + k - (NU if b_last and g == NG - 1 else 0)), k % 2

        block = ctx.enter_context(nc.Block())

        @block.sync
        def _(sp):
            sp.dma_start(wqkv_n[:], w_qkv.rearrange("(r p) d -> p r d", p=P)).then_inc(w_loaded["qkv"], 16)
            for c in range(2):
                sp.dma_start(x_sb[c][:], x_tiles[:, c * TILES:(c + 1) * TILES, :]).then_inc(x_loaded[c], 16)
            sp.dma_start(wproj_n[:], w_proj.rearrange("(r p) d -> p r d", p=P)).then_inc(w_loaded["proj"], 16)
            sp.dma_start(wgate_n[:], w_gate.rearrange("(r p) d -> p r d", p=P)).then_inc(w_loaded["gate"], 16)
            sp.dma_start(wup_n[:], w_up.rearrange("(r p) d -> p r d", p=P)).then_inc(w_loaded["up"], 16)
            sp.dma_start(wdown_n[:], w_down.rearrange("(r p) d -> p r d", p=P)).then_inc(w_loaded["down"], 16)

            def chunk_a(c, i, par, load):
                if load:
                    sp.wait_ge(xt_ready, 2 * c + 2)
                    sp.dma_start(x_sb[par][:], x_tiles[:, bass.ds((c + 2) * TILES, TILES), :]).then_inc(x_loaded[par], 16)
                for m in range(4):
                    sp.wait_ge(part2_done, 4 * c + 2 + m + 1)
                    sp.dma_start(
                        qk_dram[m // 2, :, (m % 2) * P:(m % 2 + 1) * P, bass.ds(c * CH, CH)].rearrange("w r t -> r w t"),
                        parts[m][:]).then_inc(parts_stored[m], 16)
                sp.wait_ge(v_copied[0], c + 2)
                sp.wait_ge(v_copied[1], c + 2)
                sp.dma_start(v_tiles[:, bass.ds(c * TILES, TILES), :], v_sb[par][:]).then_inc(v_stored[par], 16)

            with sp.Fori(0, PAIRS_LOOPED) as i:
                for par in range(2):
                    chunk_a(2 * i + par, i, par, True)

            def load_stacks(b, g, rows=range(len(PAIRS))):
                for r in rows:
                    pair = PAIRS[r]
                    for which, stack in ((0, q_stack), (1, k_stack)):
                        src = qk_dram[which, pair[which], g * HG * DH:(g + 1) * HG * DH, bass.ds(b * T, T)]
                        sp.dma_start(stack[g][r * DH:(r + 1) * DH, :, :],
                                     src.rearrange("(j r) t -> r j t", j=HG)).then_inc(stack_loaded[g], 16)

            def load_v(b, g):
                sp.dma_start(v_flat[g % 2][:], v_tiles[:, bass.ds(b * QT, QT), g * HG * DH:(g + 1) * HG * DH]
                             ).then_inc(v_loaded[g % 2], 16)

            def load_max_rows(g):
                for part in range(3):
                    sp.dma_start(q_stack[g][ROWS + part:ROWS + part + 1, :, :].rearrange("p j (t c) -> p (j t) c", c=P),
                                 max_rows[part * NM:(part + 1) * NM, :]).then_inc(max_rows_loaded, 16)

            def store_attn(b, g, b_last, half):
                sp.wait_ge(s_free, pair_use(b, g, b_last, ("oT", half))[0] + 1 + 2)
                sp.sem_inc(sp_passed, 1)
                sp.dma_start(a_tiles[:, bass.ds(b * QT + half * HQ, HQ), g * HG * DH:(g + 1) * HG * DH],
                             attn_sb[half][:].rearrange("p t j d -> p t (j d)")).then_inc(attn_stored[half], 16)

            for m in range(4):
                sp.wait_ge(parts_stored[m], 16 * (T // CH + 1))
            for par in range(2):
                load_stacks(0, 0, range(par, len(PAIRS), 2))
                chunk_a(2 * PAIRS_LOOPED + par, PAIRS_LOOPED, par, False)
            for m in range(4):
                sp.wait_ge(parts_stored[m], 16 * (NCH + 1))
            for par in range(2):
                sp.wait_ge(v_stored[par], 16 * (NCH // 2 + 1))
            load_v(0, 0)
            load_stacks(0, 1)
            load_v(0, 1)
            load_stacks(0, 2)
            sp.wait_ge(exp_done, 3 + 1)
            load_max_rows(0)

            def group_b(b, g, b_last):
                nb, ng = (b + 1, g + 3 - NG) if g + 3 >= NG else (b, g + 3)
                if not (b_last and g + 3 >= NG):
                    sp.wait_ge(pv_done, at(b, g, NS, RING))
                    load_stacks(nb, ng)
                if not (b_last and g + 2 >= NG):
                    sp.wait_ge(v_expanded, at(b, g, 1, 1))
                    load_v(b + 1 if g + 2 >= NG else b, (g + 2) % NG)
                if not (b_last and g + 1 >= NG):
                    sp.wait_ge(exp_done, maxima_use(b, g) + 1 + 3)
                    load_max_rows((g + 1) % NG)
                for half in range(2):
                    store_attn(b, g, b_last, half)

            with sp.Fori(0, B - 1) as b:
                for g in range(NG):
                    group_b(b, g, False)
            def load_xa(c, par):
                sp.dma_start(x_sb[par][:], x_tiles[:, bass.ds(c * TILES, TILES), :]).then_inc(xa_loaded[par], 16)
                sp.dma_start(a_sb[par][:], a_tiles[:, bass.ds(c * TILES, TILES), :]).then_inc(xa_loaded[par], 16)

            for half in range(2):
                sp.wait_ge(attn_stored[half], 16 * (NG * (B - 1) + 1))
            load_xa(0, 0)
            load_xa(1, 1)
            for g in range(NG):
                group_b(B - 1, g, True)

            for half in range(2):
                sp.wait_ge(attn_stored[half], 16 * (GROUPS + 1))

            def load_behind(c, par):
                sp.wait_ge(y_done, 2 * c + 2)
                load_xa(c + 2, par)

            def store_out(c, par):
                sp.wait_ge(out_ready, c + 1)
                sp.dma_start(out_tiles[:, bass.ds(c * TILES, TILES), :], z_sb[par][:]).then_inc(out_stored[par], 16)

            load_behind(0, 0)
            with sp.Fori(0, PAIRS_C) as i:
                load_behind(2 * i + 1, 1)
                store_out(2 * i, 0)
                load_behind(2 * i + 2, 0)
                store_out(2 * i + 1, 1)
            load_behind(NCH - 3, 1)
            for c in range(NCH - 4, NCH):
                store_out(c, c % 2)
            for par in range(2):
                sp.wait_ge(out_stored[par], 16 * (NCH // 2 + 1))

        @block.gpsimd
        def _(pool):
            pool.memset(ident[:], 0.0).then_inc(consts_ready, 1)
            pool.memset(causal[:], 0.0).then_inc(consts_ready, 1)
            pool.memset(minus_half[:], -0.5)
            pool.wait_ge(consts_ready, 2)
            pool.affine_select(out=ident[:], in_=ident[:], compare_op=ALU.not_equal, fill=1.0, base=0,
                               pattern=[[-1, P]], channel_multiplier=1).then_inc(consts_ready, 1)
            pool.affine_select(out=causal[:, T - P:T], in_=causal[:, T - P:T], compare_op=ALU.is_ge, fill=LOWEST,
                               base=0, pattern=[[-1, P]], channel_multiplier=1).then_inc(consts_ready, 1)
            pool.wait_ge(consts_ready, 4)
            pool.tensor_copy(ident_bf[:], ident[:]).then_inc(consts_ready, 1)
            pool.wait_ge(consts_ready, 5)
            for i in range(2):
                pool.memset(v_ones[i][:, :, :, DH:32], 1.0).then_inc(preset, 1)
                pool.wait_ge(preset, i + 1)
            for g in range(4):
                pool.memset(k_stack[g][ROWS:ROWS_M, :, :], -1.0).then_inc(preset, 1)
                pool.wait_ge(preset, 2 + g + 1)

            def expand_v(b, g):
                pool.wait_ge(v_loaded[g % 2], 16 * (2 * b + g // 2 + 1))
                pool.sem_inc(pool_passed, 1)
                pool.tensor_copy(v_ones[g % 2][:, :, :, 0:DH],
                                 v_flat[g % 2][:].rearrange("p t (j d) -> p t j d", j=HG)).then_inc(v_expanded, 1)

            expand_v(0, 0)

            def mask(s, uses):
                pool.wait_ge(exp_done, uses + 3)
                pool.sem_inc(pool_passed, 1)
                tile = probs[s % RING][:, :, 0:P]
                pool.affine_select(out=tile, in_=tile, compare_op=ALU.is_ge, fill=0.0, base=0,
                                   pattern=[[0, HG], [1, P]], channel_multiplier=-1).then_inc(masked, 1)

            for s in range(AHEAD):
                mask(s, bank_use(0, 0, False, HG * s + HG - 1) + 1)

            def group_b(b, g, b_last):
                last_group = b_last and g == NG - 1
                for d, s in enumerate(s for s in range(AHEAD, NS if last_group else NS + AHEAD) if s % NS in diagonal):
                    if d == 1 and not last_group:
                        pool.wait_ge(pv_done, at(b, g, NS, RING))
                        expand_v(b + 1 if g == NG - 1 else b, (g + 1) % NG)
                    mask(s, bank_use(b, g, b_last, HG * s + HG - 1) + 1)

            with pool.Fori(0, B - 1) as b:
                for g in range(NG):
                    group_b(b, g, False)
            for g in range(NG):
                group_b(B - 1, g, True)

            pool.sem_inc(h_lo_done, 3)

            def inverse_deviation(ln, step, c):
                pool.wait_ge(step, 3 * c + 3)
                pool.tensor_tensor(rstd[:, ln, :], var_eps[:, ln, :], minus_half[:],
                                   ALU.pow).then_inc(rstd_done[ln], 1)

            def chunk_c(c, has_prev, has_next):
                for hc in range(HC):
                    if hc == 2 and has_next:
                        inverse_deviation(0, ln1_step, c + 1)
                    pool.wait_ge(h_hi_done, HC * c + hc + 1)
                    pool.tensor_tensor(h_lo[:, hc, :], h_sb[hc % 3][:], h_hi[:, hc, :],
                                       ALU.subtract).then_inc(h_lo_done, 1)
                if has_prev:
                    inverse_deviation(1, ln2_step, c - 1)

            inverse_deviation(0, ln1_step, 0)
            chunk_c(0, False, True)
            with pool.Fori(1, NCH - 1) as c:
                chunk_c(c, True, True)
            chunk_c(NCH - 1, True, False)
            inverse_deviation(1, ln2_step, NCH - 1)

        @block.scalar
        def _(act):
            for u in range(0, len(units), 2):
                act.wait_ge(wt_ready, u + 1)
                act.copy(units[u][2], unit_bank(u)).then_inc(wt_copied[0], 1)

            act.sem_inc(xt_copied[0], 1)
            act.sem_inc(part1_done, 2)
            act.sem_inc(v_copied[0], 1)
            for m in range(4):
                act.sem_inc(parts_stored[m], 16)

            def copy_xt(c, par):
                act.wait_ge(xt_ready, 2 * c + 1)
                act.wait_ge(v_ready, 2 * c + 2)
                act.copy(x_t[par][:, 0, :], ps[:, 0, :]).then_inc(xt_copied[0], 1)

            def part0(c, m):
                act.wait_ge(qk_ready, 4 * c + m + 1)
                act.wait_ge(parts_stored[m], 16 * c + 16)
                act.copy(parts[m][:, 0, :], ps[:, 2 + m, :]).then_inc(part0_done, 1)

            def part1(c, m):
                act.wait_ge(qk_bank_free, 4 * c + 4 + m + 1)
                act.copy(parts[m][:, 1, :], rest[m % 2][:]).then_inc(part1_done, 1)

            def chunk_a(c, i, par, has_next):
                if has_next:
                    copy_xt(c + 1, 1 - par)
                part0(c, 0)
                part0(c, 1)
                part1(c, 0)
                part0(c, 2)
                part1(c, 1)
                part0(c, 3)
                part1(c, 2)
                part1(c, 3)
                act.wait_ge(v_ready, 2 * c + 4 + 1)
                act.wait_ge(v_stored[par], 16 * i + 16)
                act.copy(v_sb[par][:, 0:2, :].rearrange("p t d -> p (t d)"), ps[:, 6, :]).then_inc(v_copied[0], 1)

            copy_xt(0, 0)
            with act.Fori(0, PAIRS_LOOPED) as i:
                for par in range(2):
                    chunk_a(2 * i + par, i, par, True)
            for par in range(2):
                chunk_a(2 * PAIRS_LOOPED + par, PAIRS_LOOPED, par, par == 0)

            act.sem_inc(exp_done, 3)
            act.sem_inc(o_copied, 1)

            def copy_max_rows(turned):
                act.wait_ge(max_turned, turned)
                act.copy(max_rows[:], bank_bf(4)[0:3 * NM, 0:P]).then_inc(exp_done, 1)

            copy_max_rows(1)

            def exponential(n, st, pv):
                s, j = divmod(n, HG)
                w = slots[s % NS][2] * P
                act.wait_ge(st_ready, st + 1)
                if j == 0:
                    act.wait_ge(pv_done, pv)
                act.activation(probs[s % RING][:, j, 0:w], ps[:, 4 + n % 3, 0:w], ACT.Exp,
                               scale=SOFT_SCALE).then_inc(exp_done, 1)

            for n in range(HG * AHEAD):
                exponential(n, n, n // HG + 1)

            def group_b(b, g, b_last):
                def copy_o(half):
                    act.wait_ge(pv_done, at(b, g, NS, RING + HALF_END[half] + 1))
                    act.wait_ge(recip_done, at(b, g, 2, 1 + half))
                    act.copy(o_sb[:], ps[:, 7, :]).then_inc(o_copied, 1)

                for step in group_steps(b_last, g):
                    if step[0] == "st":
                        _, s, j = step
                        exponential(HG * s + j, at(b, g, NE, HG * s + j), at(b, g, NS, s + 1))
                    elif step[0] == "oC":
                        copy_o(step[1])
                    elif step[0] == "mT":
                        act.wait_ge(max_rows_loaded, at(b, g, 48, 48))
                        copy_max_rows(at(b, g, 1, 2))

            with act.Fori(0, B - 1) as b:
                for g in range(NG):
                    group_b(b, g, False)
            for g in range(NG):
                group_b(B - 1, g, True)

            def copy_at(c):
                act.wait_ge(at_ready, 2 * c + 1)
                act.wait_ge(proj_ready, 2 * c + 2)
                act.copy(a_t[:, 0, :], ps[:, 0, :]).then_inc(at_copied[0], 1)

            def x1_high(c):
                for kc in range(KC):
                    act.wait_ge(x1t_ready, 2 * c + kc + 1)
                    act.copy(x1_hi[:, kc, :], ps[:, kc, :]).then_inc(x1_hi_done, 1)

            def chunk_c(c):
                for hc in range(HC + 1):
                    if hc < HC:
                        act.wait_ge(gate_ready, HC * c + hc + 1)
                        act.wait_ge(h_done, HC * c + hc + 1)
                        act.activation(silu[hc % 2][:], ps[:, 4 + 2 * (hc % 2), :], ACT.Silu,
                                       scale=W_SCALE).then_inc(silu_done, 1)
                    if hc >= 1:
                        if hc == 1:
                            act.wait_ge(down_ready, 2 * c + 2)
                        act.wait_ge(h_done, HC * c + 2 + hc)
                        act.copy(h_hi[:, hc - 1, :], h_sb[(hc - 1) % 3][:]).then_inc(h_hi_done, 1)

            copy_at(0)
            x1_high(0)
            copy_at(1)
            with act.Fori(0, NCH - 2) as c:
                chunk_c(c)
                x1_high(c + 1)
                copy_at(c + 2)
            chunk_c(NCH - 2)
            x1_high(NCH - 1)
            chunk_c(NCH - 1)

        @block.vector
        def _(dve):
            for name, n_, b_ in (("gate", wgate_n, wgate_b), ("up", wup_n, wup_b), ("down", wdown_n, wdown_b)):
                dve.wait_ge(w_loaded[name], 16)
                dve.tensor_copy(b_[:], n_[:]).then_inc(w_cast, 1)
            for u in range(1, len(units), 2):
                dve.wait_ge(wt_ready, u + 1)
                dve.tensor_copy(units[u][2], unit_bank(u)).then_inc(wt_copied[1], 1)

            dve.sem_inc(xt_copied[1], 1)
            dve.sem_inc(qk_bank_free, 4)
            dve.sem_inc(part2_done, 2)
            dve.sem_inc(v_copied[1], 1)
            for par in range(2):
                dve.sem_inc(v_stored[par], 16)

            def copy_xt(c, par):
                dve.wait_ge(xt_ready, 2 * c + 2)
                dve.wait_ge(v_ready, 2 * c + 2)
                dve.tensor_copy(x_t[par][:, 1, :], ps[:, 1, :]).then_inc(xt_copied[1], 1)

            def rest_of(c, m):
                dve.wait_ge(part0_done, 4 * c + m + 1)
                dve.wait_ge(part1_done, 4 * c + m + 1)
                dve.wait_ge(part2_done, 4 * c + m + 1)
                dve.tensor_tensor(rest[m % 2][:], ps[:, 2 + m, :], parts[m][:, 0, :],
                                  ALU.subtract).then_inc(qk_bank_free, 1)

            def part2(c, m):
                dve.wait_ge(part1_done, 4 * c + 2 + m + 1)
                dve.tensor_tensor(parts[m][:, 2, :], rest[m % 2][:], parts[m][:, 1, :],
                                  ALU.subtract).then_inc(part2_done, 1)

            def chunk_a(c, i, par, has_next):
                if has_next:
                    copy_xt(c + 1, 1 - par)
                rest_of(c, 0)
                rest_of(c, 1)
                part2(c, 0)
                rest_of(c, 2)
                part2(c, 1)
                rest_of(c, 3)
                part2(c, 2)
                part2(c, 3)
                dve.wait_ge(v_ready, 2 * c + 4 + 2)
                dve.wait_ge(v_stored[par], 16 * i + 16)
                dve.tensor_copy(v_sb[par][:, 2:4, :].rearrange("p t d -> p (t d)"),
                                ps[:, 7, :]).then_inc(v_copied[1], 1)

            copy_xt(0, 0)
            with dve.Fori(0, PAIRS_LOOPED) as i:
                for par in range(2):
                    chunk_a(2 * i + par, i, par, True)
            for par in range(2):
                chunk_a(2 * PAIRS_LOOPED + par, PAIRS_LOOPED, par, par == 0)

            dve.sem_inc(s_free, 2)
            dve.sem_inc(recip_done, 1)
            for half in range(2):
                dve.sem_inc(attn_stored[half], 16)
            dve.wait_ge(consts_ready, 5)

            def row_maxima(use, pair, u):
                dve.wait_ge(s_ready, use + 1)
                dve.sem_inc(dve_passed, 1)
                k0 = 0
                for j, qt in max_units[u]:
                    w = (qt + 1) * P
                    scores = ps[:, 2 * pair:2 * pair + 2, :].rearrange("p a b -> p (a b)")[:, k0:k0 + w]
                    last = dve.tensor_tensor_reduce(scores, scores, causal[:, T - w:T], 1.0, LOWEST, ALU.add, ALU.max,
                                                    row_max[:, j * QT + qt:j * QT + qt + 1])
                    k0 += w
                last.then_inc(s_free, 1)

            def split_max(count, uses, k):
                a = dve
                a.wait_ge(s_free, uses + 2)
                if k:
                    a.wait_ge(max_turned, count)
                a.tensor_copy(max_parts[:, 0, :], row_max[:]).then_inc(max_step, 1)
                a.wait_ge(max_step, 4 * count + 1)
                a.tensor_tensor(max_rest[:, 0, :], row_max[:], max_parts[:, 0, :], ALU.subtract).then_inc(max_step, 1)
                a.wait_ge(max_step, 4 * count + 2)
                a.tensor_copy(max_parts[:, 1, :], max_rest[:, 0, :]).then_inc(max_step, 1)
                a.wait_ge(max_step, 4 * count + 3)
                a.tensor_tensor(max_rest[:, 1, :], max_rest[:, 0, :], max_parts[:, 1, :], ALU.subtract).then_inc(max_step, 1)
                a.wait_ge(max_step, 4 * count + 4)
                a.tensor_copy(max_parts[:, 2, :], max_rest[:, 1, :]).then_inc(max_parts_ready, 1)

            for k in range(2):
                for u in range(NU):
                    row_maxima(NU * k + u, u % 2, u)
                split_max(k, NU * (k + 1), k)

            def group_b(b, g, b_last):
                def normalise(use, pair, half):
                    turned = ps[:, 2 * pair, :].rearrange("p (t j e) -> p t j e", t=HQ, j=HG)
                    dve.wait_ge(s_ready, use + 1)
                    dve.reciprocal(recip[:, half], turned[:, :, :, DH]).then_inc(recip_done, 1)
                    dve.wait_ge(recip_done, at(b, g, 2, 1 + half + 1))
                    dve.wait_ge(attn_stored[half], at(b, g, 16, 16))
                    dve.tensor_tensor(attn_sb[half][:], turned[:, :, :, 0:DH],
                                      recip[:, half].unsqueeze(3).to_broadcast([P, HQ, HG, DH]),
                                      ALU.mult).then_inc(s_free, 1)

                for step in group_steps(b_last, g):
                    if step[0] == "max":
                        use, pair = pair_use(b, g, b_last, step)
                        row_maxima(use, pair, step[1])
                        if step[1] == NU - 1:
                            split_max(at(b, g, 1, 2), use + 1, 1)
                    elif step[0] == "oT":
                        normalise(*pair_use(b, g, b_last, step), step[1])

            with dve.Fori(0, B - 1) as b:
                for g in range(NG):
                    group_b(b, g, False)
            for g in range(NG):
                group_b(B - 1, g, True)

            dve.sem_inc(x1_lo_done, 2)
            dve.sem_inc(h_done, 2)
            dve.sem_inc(z_done, 2)
            for par in range(2):
                dve.sem_inc(out_stored[par], 16)

            def copy_at(c):
                dve.wait_ge(at_ready, 2 * c + 2)
                dve.wait_ge(proj_ready, 2 * c + 2)
                dve.tensor_copy(a_t[:, 1, :], ps[:, 1, :]).then_inc(at_copied[1], 1)

            def y_bank(c, i, par, k):
                if k == 0:
                    dve.wait_ge(xa_loaded[par], 32 * i + 32)
                dve.wait_ge(proj_ready, 2 * c + 2 + k + 1)
                dve.tensor_tensor(x1[par][:, 2 * k:2 * k + 2, :].rearrange("p t d -> p (t d)"), ps[:, 2 + k, :],
                                  x_sb[par][:, 2 * k:2 * k + 2, :].rearrange("p t d -> p (t d)"),
                                  ALU.add).then_inc(y_done, 1)

            def ln_stats(ln, step, c, buf, tiles):
                for t in tiles:
                    last = dve.bn_stats(stats[:, ln, t, :], buf[:, t, :])
                if TILES - 1 in tiles:
                    last.then_inc(step, 1)

            def ln_variance(ln, step, c):
                dve.wait_ge(step, 3 * c + 1)
                dve.sem_inc(dve_passed, 1)
                for t in range(TILES):
                    last = dve.bn_aggr(mean_var[:, ln, t, :], stats[:, ln, t, :])
                last.then_inc(step, 1)
                dve.wait_ge(step, 3 * c + 2)
                dve.tensor_scalar(var_eps[:, ln, :], mean_var[:, ln, :, 1], EPS, None, ALU.add).then_inc(step, 1)

            def ln_apply(ln, c, buf, done):
                dve.wait_ge(rstd_done[ln], c + 1)
                for t in range(TILES):
                    last = dve.tensor_scalar(buf[:, t, :], buf[:, t, :], mean_var[:, ln, t, 0:1],
                                             rstd[:, ln, t:t + 1], ALU.subtract, ALU.mult)
                last.then_inc(done, 1)

            def z_banks(c, i, par):
                for k in range(2):
                    dve.wait_ge(down_ready, 2 * c + 2 + k + 1)
                    if k == 0:
                        dve.wait_ge(out_stored[par], 16 * i + 16)
                    dve.scalar_tensor_tensor(out=z_sb[par][:, 2 * k:2 * k + 2, :].rearrange("p t d -> p (t d)"),
                                             in0=ps[:, 2 + k, :], scalar=2.0 * W_SCALE,
                                             in1=x1[par][:, 2 * k:2 * k + 2, :].rearrange("p t d -> p (t d)"),
                                             op0=ALU.mult, op1=ALU.add).then_inc(z_done, 1)

            def x1_low(c):
                for kc in range(KC):
                    dve.wait_ge(x1_hi_done, 2 * c + kc + 1)
                    dve.tensor_tensor(x1_lo[:, kc, :], ps[:, kc, :], x1_hi[:, kc, :],
                                      ALU.subtract).then_inc(x1_lo_done, 1)

            def hidden(c, hc):
                dve.wait_ge(silu_done, HC * c + hc + 1)
                dve.wait_ge(up_ready, HC * c + hc + 1)
                dve.wait_ge(h_lo_done, HC * c + hc + 1)
                dve.scalar_tensor_tensor(out=h_sb[hc % 3][:], in0=ps[:, 5 + 2 * (hc % 2), :], scalar=0.5 * W_SCALE,
                                         in1=silu[hc % 2][:], op0=ALU.mult, op1=ALU.mult).then_inc(h_done, 1)

            def chunk_c(c, i, par, has_prev, has_next, has_third):
                n, ni, npar = c + 1, i + par, 1 - par
                if has_prev:
                    z_banks(c - 1, i + par - 1, npar)
                hidden(c, 0)
                if has_next:
                    y_bank(n, ni, npar, 0)
                    y_bank(n, ni, npar, 1)
                hidden(c, 1)
                if has_next:
                    dve.wait_ge(y_done, 2 * n + 2)
                    ln_stats(0, ln1_step, n, x1[npar], range(TILES))
                    ln_variance(0, ln1_step, n)
                hidden(c, 2)
                hidden(c, 3)
                if has_next:
                    ln_apply(0, n, x1[npar], x1_ready)
                hidden(c, 4)
                hidden(c, 5)
                if has_next:
                    x1_low(n)
                if has_prev:
                    dve.wait_ge(z_done, 2 * c + 2)
                    ln_stats(1, ln2_step, c - 1, z_sb[npar], range(TILES))
                    ln_variance(1, ln2_step, c - 1)
                if has_third:
                    copy_at(c + 2)
                if has_prev:
                    ln_apply(1, c - 1, z_sb[npar], out_ready)

            copy_at(0)
            y_bank(0, 0, 0, 0)
            y_bank(0, 0, 0, 1)
            dve.wait_ge(y_done, 2)
            ln_stats(0, ln1_step, 0, x1[0], range(TILES))
            ln_variance(0, ln1_step, 0)
            ln_apply(0, 0, x1[0], x1_ready)
            x1_low(0)
            copy_at(1)
            chunk_c(0, 0, 0, False, True, True)
            with dve.Fori(0, PAIRS_C) as i:
                chunk_c(2 * i + 1, i, 1, True, True, True)
                chunk_c(2 * i + 2, i + 1, 0, True, True, True)
            for c in range(NCH - 3, NCH):
                chunk_c(c, c // 2, c % 2, True, c < NCH - 1, c < NCH - 2)
            z_banks(NCH - 1, PAIRS_LOOPED, 1)
            dve.wait_ge(z_done, 2 * NCH + 2)
            ln_stats(1, ln2_step, NCH - 1, z_sb[1], range(TILES))
            ln_variance(1, ln2_step, NCH - 1)
            ln_apply(1, NCH - 1, z_sb[1], out_ready)

        @block.tensor
        def _(pe):
            pe.wait_ge(consts_ready, 5)
            for u, (name, tiles, dst) in enumerate(units):
                pe.wait_ge(w_loaded[name], 16)
                if name in casts:
                    pe.wait_ge(w_cast, casts[name])
                if u >= 8:
                    pe.wait_ge(wt_copied[u % 2], (u - 8) // 2 + 1)
                bank = unit_bank(u)
                for n, tile in enumerate(tiles):
                    last = pe.transpose(bank[:, tile_cols(n)], tile, ident_bf[:] if name in casts else ident[:])
                last.then_inc(wt_ready, 1)
            pe.wait_ge(wt_copied[0], (len(units) + 1) // 2)
            pe.wait_ge(wt_copied[1], len(units) // 2)

            pe.sem_inc(v_ready, 4)

            def turn_x(c, i, par):
                pe.wait_ge(x_loaded[par], 16 * i + 16)
                for kc in range(KC):
                    pe.wait_ge(xt_copied[kc], c + 1)
                    for t in range(TILES):
                        last = pe.transpose(ps[:, kc, tile_cols(t)], x_sb[par][:, t, kc * P:(kc + 1) * P], ident[:])
                    last.then_inc(xt_ready, 1)

            def chunk_a(c, i, par, has_next):
                if has_next:
                    turn_x(c + 1, i + par, 1 - par)
                pe.wait_ge(xt_copied[0], c + 2)
                pe.wait_ge(xt_copied[1], c + 2)
                for m in range(4):
                    pe.wait_ge(qk_bank_free, 4 * c + m + 1)
                    for kc in range(KC):
                        last = pe.matmul(ps[:, 2 + m, :], wqkv_t[:, kc, m * P:(m + 1) * P], x_t[par][:, kc, :],
                                         start=kc == 0, stop=kc == KC - 1)
                    last.then_inc(qk_ready, 1)
                for k in range(2):
                    pe.wait_ge(v_copied[k], c + 1)
                    for t in (2 * k, 2 * k + 1):
                        for kc in range(KC):
                            last = pe.matmul(ps[:, 6 + k, (t % 2) * D:(t % 2 + 1) * D], x_t[par][:, kc, tile_cols(t)],
                                             wqkv_t[:, kc, 2 * D:3 * D], start=kc == 0, stop=kc == KC - 1)
                    last.then_inc(v_ready, 1)

            turn_x(0, 0, 0)
            with pe.Fori(0, PAIRS_LOOPED) as i:
                for par in range(2):
                    chunk_a(2 * i + par, i, par, True)
            for par in range(2):
                chunk_a(2 * PAIRS_LOOPED + par, PAIRS_LOOPED, par, par == 0)
            for k in range(2):
                pe.wait_ge(xt_copied[k], NCH + 1)
                pe.wait_ge(v_copied[k], NCH + 1)
            pe.wait_ge(qk_bank_free, 4 * NCH + 4)

            pe.wait_ge(preset, 6)

            pe.sem_inc(pv_done, RING)

            def scores_for_max(g, use, pair, u):
                pe.wait_ge(s_free, use + 1)
                c0 = 0
                for j, qt in max_units[u]:
                    k0, k_end = 0, (qt + 1) * P
                    while k0 < k_end:
                        w = min(CH - c0 % CH, k_end - k0)
                        last = pe.matmul(ps[:, 2 * pair + c0 // CH, c0 % CH:c0 % CH + w],
                                         q_stack[g][0:ROWS, j, tile_cols(qt)], k_stack[g][0:ROWS, j, k0:k0 + w],
                                         start=True, stop=True)
                        k0, c0 = k0 + w, c0 + w
                last.then_inc(s_ready, 1)

            def turn_max(ready, use):
                pe.wait_ge(max_parts_ready, ready)
                if use is not None:
                    pe.wait_ge(exp_done, use)
                pe.transpose(bank_bf(4)[0:3 * NM, 0:P], max_parts[:].rearrange("p a m -> p (a m)"),
                             ident_bf[:]).then_inc(max_turned, 1)

            for k in range(2):
                pe.wait_ge(stack_loaded[k], 16 * 12)
                for u in range(NU):
                    scores_for_max(k, NU * k + u, u % 2, u)
                    if k == 1 and u == 1:
                        turn_max(1, None)

            def scores(g, n, before):
                s, j = divmod(n, HG)
                half, kt, w = slots[s]
                q0 = max(half * HQ, kt) * P
                pe.wait_ge(exp_done, before + 1 + 3)
                pe.matmul(ps[:, 4 + n % 3, 0:w * P], k_stack[g][0:ROWS_M, j, tile_cols(kt)],
                          q_stack[g][0:ROWS_M, j, q0:q0 + w * P], start=True, stop=True).then_inc(st_ready, 1)

            pe.wait_ge(max_rows_loaded, 48)
            for n in range(HG * AHEAD):
                scores(0, n, bank_use(0, 0, False, n - 3))

            def group_b(b, g, b_last):
                for step in group_steps(b_last, g):
                    if step[0] == "st":
                        _, s, j = step
                        if s == NS and j == 0:
                            pe.wait_ge(max_rows_loaded, at(b, g, 48, 96))
                        n = HG * s + j
                        behind_maxima = n == HG * (AHEAD + 1) and not (b_last and g == NG - 1)
                        scores((g + s // NS) % NG, n % NE,
                               maxima_use(b, g) if behind_maxima else bank_use(b, g, b_last, n - 3))
                    elif step[0] == "pv":
                        s = step[1]
                        half, kt, w = slots[s]
                        c0 = (max(half * HQ, kt) - half * HQ) * P
                        if s == 0:
                            pe.wait_ge(v_expanded, at(b, g, 1, 1))
                        if kt == 0:
                            pe.wait_ge(o_copied, at(b, g, 2, 1 + half))
                        if s in diagonal:
                            pe.wait_ge(masked, at(b, g, ND, diagonal.index(s) + 1))
                        else:
                            pe.wait_ge(exp_done, bank_use(b, g, b_last, HG * s + HG - 1) + 1 + 3)
                        for j in range(HG):
                            last = pe.matmul(ps[32 * j:32 * j + 32, 7, c0:c0 + w * P], v_ones[g % 2][:, kt, j, :],
                                             probs[s % RING][:, j, 0:w * P], start=kt == 0, stop=s == HALF_END[half])
                        last.then_inc(pv_done, 1)
                    elif step[0] == "max":
                        if step[1] == 0:
                            pe.wait_ge(stack_loaded[(g + 2) % NG], 192 * (b + (g + 2) // NG + 1))
                        scores_for_max((g + 2) % NG, *pair_use(b, g, b_last, step), step[1])
                    elif step[0] == "mT":
                        turn_max(at(b, g, 1, 2), bank_use(b, g, b_last, HG * (AHEAD + 1) - 3) + 1 + 3)
                    elif step[0] == "oT":
                        half = step[1]
                        pe.wait_ge(o_copied, at(b, g, 2, 1 + half + 1))
                        use, pair = pair_use(b, g, b_last, step)
                        pe.wait_ge(s_free, use + 1)
                        for t in range(HQ):
                            last = pe.transpose(ps[:, 2 * pair, tile_cols(t)], o_sb[:, tile_cols(t)], ident[:])
                        last.then_inc(s_ready, 1)

            with pe.Fori(0, B - 1) as b:
                for g in range(NG):
                    group_b(b, g, False)
            for g in range(NG):
                group_b(B - 1, g, True)
            pe.wait_ge(s_free, 2 + NP * GROUPS)
            pe.wait_ge(exp_done, 3 + NR * GROUPS)
            pe.wait_ge(o_copied, 1 + 2 * GROUPS)

            pe.sem_inc(proj_ready, 2)
            pe.sem_inc(down_ready, 2)

            def turn_attn(c, i, par):
                pe.wait_ge(xa_loaded[par], 32 * i + 32)
                pe.wait_ge(x1_lo_done, 2 * c + 2)
                for kc in range(KC):
                    for t in range(TILES):
                        last = pe.transpose(ps[:, kc, tile_cols(t)], a_sb[par][:, t, kc * P:(kc + 1) * P], ident[:])
                    last.then_inc(at_ready, 1)

            def project(c):
                pe.wait_ge(at_copied[0], c + 1)
                pe.wait_ge(at_copied[1], c + 1)
                for t in range(TILES):
                    for kc in range(KC):
                        last = pe.matmul(ps[:, 2 + t // 2, (t % 2) * D:(t % 2 + 1) * D], a_t[:, kc, tile_cols(t)],
                                         wproj_t[:, kc, :], start=kc == 0, stop=kc == KC - 1)
                    if t % 2:
                        last.then_inc(proj_ready, 1)

            def turn_x1(c, par):
                pe.wait_ge(x1_ready, c + 1)
                for kc in range(KC):
                    for t in range(TILES):
                        last = pe.transpose(ps[:, kc, tile_cols(t)], x1[par][:, t, kc * P:(kc + 1) * P], ident[:])
                    last.then_inc(x1t_ready, 1)

            def chunk_c(c, i, par, has_next, has_third):
                pe.wait_ge(x1_lo_done, 2 * c + 4)
                for hc in range(HC):
                    if hc == 1 and has_next:
                        pe.wait_ge(z_done, 2 * c + 2)
                        project(c + 1)
                    pe.wait_ge(h_done, HC * c + hc + 1)
                    for w, bank, ready in ((wgate_t, 4, gate_ready), (wup_t, 5, up_ready)):
                        for kc in range(KC):
                            for part in (x1_hi, x1_lo):
                                last = pe.matmul(ps[:, bank + 2 * (hc % 2), :], w[:, kc, hc * P:(hc + 1) * P], part[:, kc, :],
                                                 start=kc == 0 and part is x1_hi, stop=kc == KC - 1 and part is x1_lo)
                        last.then_inc(ready, 1)
                if has_next:
                    turn_x1(c + 1, 1 - par)
                    pe.wait_ge(y_done, 2 * c + 4)
                for hc in range(HC):
                    if hc == 4 and has_third:
                        turn_attn(c + 2, i + 1, par)
                    pe.wait_ge(h_lo_done, HC * c + 3 + hc + 1)
                    for t in range(TILES):
                        for part in (h_hi, h_lo):
                            last = pe.matmul(ps[:, 2 + t // 2, (t % 2) * D:(t % 2 + 1) * D], part[:, hc, tile_cols(t)],
                                             wdown_t[:, hc, :], start=hc == 0 and part is h_hi and t % 2 == 0,
                                             stop=hc == HC - 1 and part is h_lo, skip_group_check=True)
                        if hc == HC - 1 and t % 2:
                            last.then_inc(down_ready, 1)

            turn_attn(0, 0, 0)
            project(0)
            turn_x1(0, 0)
            turn_attn(1, 0, 1)
            chunk_c(0, 0, 0, True, True)
            with pe.Fori(0, PAIRS_C) as i:
                chunk_c(2 * i + 1, i, 1, True, True)
                chunk_c(2 * i + 2, i + 1, 0, True, True)
            for c in range(NCH - 3, NCH):
                chunk_c(c, c // 2, c % 2, c < NCH - 1, c < NCH - 2)


_INS = ["L0_attn_x", "L0_attn_W_qkv", "L0_attn_W_proj", "L0_ffn_w_gate", "L0_ffn_w_up", "L0_ffn_w_down"]


def kernel(**inputs):
    import numpy as _np
    import concourse.bacc as _bacc
    from concourse import mybir as _mybir
    from concourse.bass_utils import run_bass_kernel_spmd as _run

    nc = _bacc.Bacc("TRN2", target_bir_lowering=False, num_devices=1)
    arrays, args = {}, []
    for name in _INS:
        a = _np.ascontiguousarray(inputs[name])
        arrays[f"in_{name}"] = a
        args.append(nc.dram_tensor(f"in_{name}", a.shape, _mybir.dt.from_np(a.dtype), kind="ExternalInput").ap())
    out = nc.dram_tensor("out_x", inputs["L0_attn_x"].shape, F32, kind="ExternalOutput").ap()
    block_kernel(nc, *args, out)
    r = _run(nc, [arrays], core_ids=[0])
    return r.results[0]["out_x"]
```

```python
from contextlib import ExitStack

import concourse.bass as bass
from concourse import mybir

F32 = mybir.dt.float32
BF16 = mybir.dt.bfloat16
F16 = mybir.dt.float16
I32 = mybir.dt.int32
ALU = mybir.AluOpType
ACT = mybir.ActivationFunctionType


RING = 3


def attention_steps(slots, diagonal, unit_items, ahead, units_from, units_to, has_next):
    COLS, EXP, ROW_MAX, PV, TURN = 54, (50, 107), (68, 134), (110, 214), 428
    MASK, COPY, COPY_ROWS, NORMALISE, SPLIT = 594, 478, 158, 650, 950
    PE_ACT, PE_DVE, ACT_PE, DVE_PE, ACT_POOL, POOL_PE = 240, 330, 150, 230, 230, 180
    ROWS_MOVED = 2700
    LEAD_ST = 0.03
    ns, nu, hg = len(slots), len(unit_items), 4
    whole = hg * sum(w for _, _, w in slots)
    pe = act = dve = pool = o_free = 0
    st_free, s_free = [0, 0, 0], [0, 0]
    pv_ready, pairs_used, parts_ready, rows_ready = {s: 0 for s in range(ahead)}, 0, 0, 0
    for turn in range(4):
        n, end, m, p = hg * ahead, hg * (ns + ahead * has_next), units_from, 0
        st_cols = max_cols = pv_cols = 0
        turns, order, pv_end, next_ready = [], [], {}, {}
        while n < end or p < ns or turns or m < units_to:
            could = []
            rows_due = has_next and ("mT",) not in order
            if rows_due and m >= nu:
                could.append((max(st_free[n % 3], parts_ready), -1, "mT"))
            if n < end and n // hg < p + RING and not (rows_due and n >= hg * ns):
                could.append((max(st_free[n % 3], rows_ready if n == hg * ns else 0), st_cols / whole - LEAD_ST, "st"))
            if m < units_to:
                could.append((s_free[pairs_used % 2], max_cols / whole, "max"))
            if p < ns and p in pv_ready:
                could.append((max(pv_ready[p], o_free if slots[p][1] == 0 else 0), pv_cols / whole, "pv"))
            if turns:
                could.append((max(turns[0][1], s_free[pairs_used % 2]), -1, "oT"))
            ready = [c for c in could if c[0] <= pe] or [min(could)]
            start, _, what = min(ready, key=lambda c: c[1])
            pe = max(pe, start)
            if what == "st":
                s, j = divmod(n, hg)
                w = slots[s % ns][2]
                order.append(("st", s, j))
                pe += max(w * COLS, 90)
                room = pv_end.get(s - RING, 0) + PE_ACT if j == 0 else 0
                act = max(act, pe + PE_ACT, room) + EXP[0] + w * EXP[1]
                st_free[n % 3] = act + ACT_PE
                n, st_cols = n + 1, st_cols + w
                if j == hg - 1:
                    ready_at = act + ACT_PE
                    if s % ns in diagonal:
                        pool = max(pool, act + ACT_POOL) + MASK
                        ready_at = pool + POOL_PE
                    (pv_ready if s < ns else next_ready)[s % ns] = ready_at
            elif what == "mT":
                order.append(("mT",))
                pe += COLS
                act = max(act, pe + PE_ACT) + COPY_ROWS
                st_free[n % 3] = act + ACT_PE
                rows_ready = act + ROWS_MOVED
            elif what == "max":
                order.append(("max", m))
                cols = sum(qt + 1 for _, qt in unit_items[m % nu])
                pe += cols * COLS
                dve = max(dve, pe + PE_DVE) + len(unit_items[m % nu]) * ROW_MAX[0] + cols * ROW_MAX[1]
                s_free[pairs_used % 2] = dve + DVE_PE
                m, max_cols, pairs_used = m + 1, max_cols + cols, pairs_used + 1
                if m == nu:
                    dve += SPLIT
                    parts_ready = dve + DVE_PE
            elif what == "pv":
                order.append(("pv", p))
                pe += PV[0] + slots[p][2] * PV[1]
                pv_end[p] = pe
                p, pv_cols = p + 1, pv_cols + hg * slots[p][2]
                if p == ns or slots[p][0] != slots[p - 1][0]:
                    half = slots[p - 1][0]
                    order.append(("oC", half))
                    act = max(act, pe + PE_ACT) + COPY
                    o_free = act + ACT_PE
                    turns.append((half, o_free))
            else:
                order.append(("oT", turns.pop(0)[0]))
                pe += TURN
                dve = max(dve, pe + PE_DVE) + NORMALISE
                s_free[pairs_used % 2] = dve + DVE_PE
                pairs_used += 1
        pv_ready = next_ready
        if not has_next or units_to < units_from + nu:
            break
    return order


def block_kernel(nc, x, w_qkv, w_proj, w_gate, w_up, w_down, out):
    P = 128
    B, T, D = x.shape
    HID = w_gate.shape[0]
    H = 16
    DH = D // H
    NTOK = B * T
    CH = 512
    NCH = NTOK // CH
    TILES = CH // P
    KC = D // P
    HC = HID // P
    QT = T // P
    HG = 4
    NG = H // HG
    GROUPS = B * NG
    EPS = 1e-5
    SOFT_SCALE = 1.0 / float(DH) ** 0.5
    W_SCALE = 1.0 / 127.0
    LOWEST = -3.0e38
    PAIRS = [(0, 0), (1, 0), (2, 0), (0, 1), (1, 1), (0, 2)]
    ROWS = len(PAIRS) * DH
    ROWS_M = ROWS + 3

    HQ = QT // 2
    slots = [(0, kt, HQ - kt) for kt in range(HQ)]
    slots += [(1, kt, min(HQ, QT - kt)) for kt in range(QT)]
    diagonal = [s for s, (half, kt, w) in enumerate(slots) if kt >= half * HQ]
    NS = len(slots)
    NE = NS * HG
    NM = HG * QT
    ND = len(diagonal)
    NR = NE + 1
    max_units = []
    for j in range(0, HG, 2):
        for k in (j, j + 1):
            max_units += [[(k, QT - 1)]] + [[(k, QT - 1 - t), (k, t - 1)] for t in range(1, QT // 2)]
        max_units.append([(j, QT // 2 - 1), (j + 1, QT // 2 - 1)])
    NU = len(max_units)
    UNITS_AHEAD = 12
    NP = NU + 2
    HALF_END = [HQ - 1, NS - 1]
    AHEAD = 2

    xf = x.rearrange("b t d -> (b t) d")
    of = out.rearrange("b t d -> (b t) d")
    x_tiles = xf.rearrange("(c p) d -> p c d", p=P)
    out_tiles = of.rearrange("(c p) d -> p c d", p=P)
    qk_dram = nc.dram_tensor("qk_parts", [2, 3, D, NTOK], BF16, kind="Internal").ap()
    v_dram = nc.dram_tensor("v_rows", [NTOK, D], F32, kind="Internal").ap()
    a_dram = nc.dram_tensor("attn_rows", [NTOK, D], F32, kind="Internal").ap()
    v_tiles = v_dram.rearrange("(c p) d -> p c d", p=P)
    a_tiles = a_dram.rearrange("(c p) d -> p c d", p=P)

    with ExitStack() as ctx:
        def sb(name, shape, dt):
            return ctx.enter_context(nc.sbuf_tensor(name, shape, dt))

        def sem(name):
            return ctx.enter_context(nc.semaphore(name))

        ps = ctx.enter_context(nc.psum_tensor("ps", [P, 8, 512], F32))

        ident = sb("ident", [P, P], F32)
        ident_bf = sb("ident_bf", [P, P], BF16)
        ident_f16 = sb("ident_f16", [P, P], F16)
        causal = sb("causal", [P, T], F32)
        minus_half = sb("minus_half", [P, TILES], F32)
        wqkv_t = sb("wqkv_t", [P, KC, 3 * D], F32)
        wproj_t = sb("wproj_t", [P, KC, D], F32)
        wgate_t = sb("wgate_t", [P, KC, HID], BF16)
        wup_t = sb("wup_t", [P, KC, HID], BF16)
        wdown_t = sb("wdown_t", [P, HC, D], BF16)

        x_sb = [sb(f"x_sb{i}", [P, TILES, D], F32) for i in range(2)]
        x_t = [sb(f"x_t{i}", [P, KC, CH], F32) for i in range(2)]
        parts = [sb(f"parts{i}", [P, 3, CH], BF16) for i in range(4)]
        rest = [sb(f"rest{i}", [P, CH], F32) for i in range(2)]
        v_sb = [sb(f"v_sb{i}", [P, TILES, D], F32) for i in range(2)]
        wproj_n = sb("wproj_n", [P, KC, D], F32)
        wgate_b = sb("wgate_b", [P, HC, D], BF16)
        wup_b = sb("wup_b", [P, HC, D], BF16)
        wdown_b = sb("wdown_b", [P, KC, HID], BF16)
        x1 = [sb(f"x1_{i}", [P, TILES, D], F32) for i in range(2)]
        stats = sb("stats", [P, 2, TILES, 6], F32)
        mean_var = sb("mean_var", [P, 2, TILES, 2], F32)
        var_eps = sb("var_eps", [P, 2, TILES], F32)
        rstd = sb("rstd", [P, 2, TILES], F32)
        with ExitStack() as early:
            def sb_early(name, shape, dt):
                return early.enter_context(nc.sbuf_tensor(name, shape, dt))

            wqkv_n = sb_early("wqkv_n", [P, 3 * KC, D], F32)
            wgate_n = sb_early("wgate_n", [P, HC, D], I32)
            wup_n = sb_early("wup_n", [P, HC, D], I32)
            wdown_n = sb_early("wdown_n", [P, KC, HID], I32)

        with ExitStack() as middle:
            def sb_middle(name, shape, dt):
                return middle.enter_context(nc.sbuf_tensor(name, shape, dt))

            q_stack = [sb_middle(f"q_stack{i}", [P, HG, T], BF16) for i in range(4)]
            v_flat = [sb_middle(f"v_flat{i}", [P, QT, HG * DH], F32) for i in range(2)]
            k_stack = [sb_middle(f"k_stack{i}", [P, HG, T], BF16) for i in range(4)]
            v_ones = [sb_middle(f"v_ones{i}", [P, QT, HG, 32], F32) for i in range(2)]
            probs = [sb_middle(f"probs{i}", [P, HG, CH], F32) for i in range(RING)]
            row_max = sb_middle("row_max", [P, NM], F32)
            max_rest = sb_middle("max_rest", [P, 2, NM], F32)
            max_parts = sb_middle("max_parts", [P, 3, NM], BF16)
            max_rows = sb_middle("max_rows", [3 * NM, P], BF16)
            o_sb = sb_middle("o_sb", [P, CH], F32)
            recip = sb_middle("recip", [P, 2, HQ, HG], F32)
            attn_sb = [sb_middle(f"attn_sb{i}", [P, HQ, HG, DH], F32) for i in range(2)]

        a_sb = v_sb
        a_t = x_t[0]
        x1_hi_rows = sb("x1_hi_rows", [P, TILES, D], F16)
        x1_lo_rows = sb("x1_lo_rows", [P, TILES, D], F16)
        x1_hi = sb("x1_hi", [P, KC, CH], F16)
        x1_lo = sb("x1_lo", [P, KC, CH], F16)
        silu = [sb(f"silu{i}", [P, CH], F32) for i in range(2)]
        h_sb = [sb(f"h_sb{i}", [P, CH], F32) for i in range(3)]
        h_hi = sb("h_hi", [P, HC, CH], F16)
        h_lo = sb("h_lo", [P, HC, CH], F16)
        z_sb = [sb(f"z_sb{i}", [P, TILES, D], F32) for i in range(2)]

        w_loaded = {n: sem(f"w_loaded_{n}") for n in ("qkv", "proj", "gate", "up", "down")}
        consts_ready = sem("consts_ready")
        preset = sem("preset")
        w_cast = sem("w_cast")
        wt_ready = sem("wt_ready")
        wt_copied = [sem("wt_copied_act"), sem("wt_copied_dve")]
        late_wt_ready = sem("late_wt_ready")
        late_wt_copied = sem("late_wt_copied")
        dve_passed = sem("dve_passed")
        pool_passed = sem("pool_passed")
        sp_passed = sem("sp_passed")
        x_loaded = [sem(f"x_loaded{i}") for i in range(2)]
        xt_ready = sem("xt_ready")
        xt_copied = [sem("xt_copied_act"), sem("xt_copied_dve")]
        qk_ready = sem("qk_ready")
        part0_done = sem("part0_done")
        qk_bank_free = sem("qk_bank_free")
        part1_done = sem("part1_done")
        part2_done = sem("part2_done")
        parts_stored = [sem(f"parts_stored{i}") for i in range(4)]
        v_ready = sem("v_ready")
        v_copied = [sem("v_copied_act"), sem("v_copied_dve")]
        v_stored = [sem(f"v_stored{i}") for i in range(2)]
        stack_loaded = [sem(f"stack_loaded{i}") for i in range(4)]
        v_loaded = [sem(f"v_loaded{i}") for i in range(2)]
        v_expanded = sem("v_expanded")
        s_ready = sem("s_ready")
        s_free = sem("s_free")
        max_step = sem("max_step")
        max_parts_ready = sem("max_parts_ready")
        max_turned = sem("max_turned")
        max_rows_loaded = sem("max_rows_loaded")
        st_ready = sem("st_ready")
        exp_done = sem("exp_done")
        masked = sem("masked")
        pv_done = sem("pv_done")
        o_copied = sem("o_copied")
        recip_done = sem("recip_done")
        attn_stored = [sem(f"attn_stored{i}") for i in range(2)]
        xa_loaded = [sem(f"xa_loaded{i}") for i in range(2)]
        at_ready = sem("at_ready")
        at_copied = [sem("at_copied_act"), sem("at_copied_dve")]
        proj_ready = sem("proj_ready")
        y_done = sem("y_done")
        ln1_step = sem("ln1_step")
        rstd_done = [sem("rstd1_done"), sem("rstd2_done")]
        x1_ready = sem("x1_ready")
        x1_hi_split = sem("x1_hi_split")
        x1_lo_split = sem("x1_lo_split")
        x1t_ready = [sem("x1t_hi_ready"), sem("x1t_lo_ready")]
        x1_done = [sem("x1_hi_done"), sem("x1_lo_done")]
        gate_ready = sem("gate_ready")
        up_ready = sem("up_ready")
        silu_done = sem("silu_done")
        h_done = sem("h_done")
        h_hi_done = sem("h_hi_done")
        h_lo_done = sem("h_lo_done")
        down_ready = sem("down_ready")
        z_done = sem("z_done")
        ln2_step = sem("ln2_step")
        out_ready = sem("out_ready")
        out_stored = [sem(f"out_stored{i}") for i in range(2)]

        def bank_bf(b):
            return ps[:, b, :].bitcast(BF16)

        def bank_f16(b):
            return ps[:, b, :].bitcast(F16).rearrange("p (k t) -> p k t", k=KC)

        units = []
        for kc in range(KC):
            for r in (0, 3):
                units.append(("qkv", [wqkv_n[:, r + i, kc * P:(kc + 1) * P] for i in range(3)],
                              wqkv_t[:, kc, r * P:(r + 3) * P]))
        for kc in range(KC):
            units.append(("proj", [wproj_n[:, r, kc * P:(kc + 1) * P] for r in range(KC)], wproj_t[:, kc, :]))
        for name, src, dst in (("gate", wgate_b, wgate_t), ("up", wup_b, wup_t)):
            for kc in range(KC):
                for r in (0, 3):
                    units.append((name, [src[:, r + i, kc * P:(kc + 1) * P] for i in range(3)],
                                  dst[:, kc, r * P:(r + 3) * P]))
        for hc in range(0, HC, 2):
            units.append(("down", [wdown_b[:, r, (hc + i) * P:(hc + i + 1) * P] for i in range(2) for r in range(KC)],
                          wdown_t[:, hc:hc + 2, :].rearrange("p a b -> p (a b)")))
        casts = {"gate": 1, "up": 2, "down": 3}

        early_units = [u for u in units if u[0] == "qkv"]
        late_units = [u for u in units if u[0] != "qkv"]

        def unit_bank(unit, b):
            name, tiles, dst = unit
            bank = bank_bf(b) if name in casts else ps[:, b, :]
            return bank[:, 0:len(tiles) * P]

        PAIRS_LOOPED = NCH // 2 - 1
        TURN_HI, TURN_LO = 1, 3
        PAIRS_C = NCH // 2 - 2

        def tile_cols(t):
            return slice(t * P, (t + 1) * P)

        def group_steps(b_last, g):
            groups_left = NG - 1 - g if b_last else NG
            units_to = UNITS_AHEAD + NU if groups_left > 1 else NU if groups_left else UNITS_AHEAD
            return attention_steps(slots, diagonal, max_units, AHEAD, UNITS_AHEAD, units_to, groups_left > 0)

        def maxima_at(b_last, g):
            steps = group_steps(b_last, g)
            if ("mT",) not in steps:
                return NE
            return HG * AHEAD + len([s for s in steps[:steps.index(("mT",))] if s[0] == "st"])

        def at(b, g, per, n):
            return b * (NG * per) + (g * per + n)

        def bank_use(b, g, b_last, n):
            return at(b, g, NR, 1 + n + (1 if n >= maxima_at(b_last, g) else 0))

        def maxima_use(b, g, b_last):
            return at(b, g, NR, 1 + maxima_at(b_last, g))

        def pair_use(b, g, b_last, step):
            k = [s for s in group_steps(b_last, g) if s[0] in ("max", "oT")].index(step)
            return at(b, g, NP, NU + UNITS_AHEAD + k - (UNITS_AHEAD if b_last and g == NG - 1 else 0)), k % 2

        block = ctx.enter_context(nc.Block())

        @block.sync
        def _(sp):
            sp.dma_start(wqkv_n[:], w_qkv.rearrange("(r p) d -> p r d", p=P)).then_inc(w_loaded["qkv"], 16)
            for c in range(2):
                sp.dma_start(x_sb[c][:], x_tiles[:, c * TILES:(c + 1) * TILES, :]).then_inc(x_loaded[c], 16)
            sp.dma_start(wproj_n[:], w_proj.rearrange("(r p) d -> p r d", p=P)).then_inc(w_loaded["proj"], 16)
            sp.dma_start(wgate_n[:], w_gate.rearrange("(r p) d -> p r d", p=P)).then_inc(w_loaded["gate"], 16)
            sp.dma_start(wup_n[:], w_up.rearrange("(r p) d -> p r d", p=P)).then_inc(w_loaded["up"], 16)
            sp.dma_start(wdown_n[:], w_down.rearrange("(r p) d -> p r d", p=P)).then_inc(w_loaded["down"], 16)

            def chunk_a(c, i, par, load):
                if load:
                    sp.wait_ge(xt_ready, 2 * c + 2)
                    sp.dma_start(x_sb[par][:], x_tiles[:, bass.ds((c + 2) * TILES, TILES), :]).then_inc(x_loaded[par], 16)
                for m in range(4):
                    sp.wait_ge(part2_done, 4 * c + 2 + m + 1)
                    sp.dma_start(
                        qk_dram[m // 2, :, (m % 2) * P:(m % 2 + 1) * P, bass.ds(c * CH, CH)].rearrange("w r t -> r w t"),
                        parts[m][:]).then_inc(parts_stored[m], 16)
                sp.wait_ge(v_copied[0], c + 2)
                sp.wait_ge(v_copied[1], c + 2)
                sp.dma_start(v_tiles[:, bass.ds(c * TILES, TILES), :], v_sb[par][:]).then_inc(v_stored[par], 16)

            with sp.Fori(0, PAIRS_LOOPED) as i:
                for par in range(2):
                    chunk_a(2 * i + par, i, par, True)

            def load_stacks(b, g, rows=range(len(PAIRS))):
                for r in rows:
                    pair = PAIRS[r]
                    for which, stack in ((0, q_stack), (1, k_stack)):
                        src = qk_dram[which, pair[which], g * HG * DH:(g + 1) * HG * DH, bass.ds(b * T, T)]
                        sp.dma_start(stack[g][r * DH:(r + 1) * DH, :, :],
                                     src.rearrange("(j r) t -> r j t", j=HG)).then_inc(stack_loaded[g], 16)

            def load_v(b, g):
                sp.dma_start(v_flat[g % 2][:], v_tiles[:, bass.ds(b * QT, QT), g * HG * DH:(g + 1) * HG * DH]
                             ).then_inc(v_loaded[g % 2], 16)

            def load_max_rows(g):
                for part in range(3):
                    sp.dma_start(q_stack[g][ROWS + part:ROWS + part + 1, :, :].rearrange("p j (t c) -> p (j t) c", c=P),
                                 max_rows[part * NM:(part + 1) * NM, :]).then_inc(max_rows_loaded, 16)

            def store_attn(b, g, b_last, half):
                sp.wait_ge(s_free, pair_use(b, g, b_last, ("oT", half))[0] + 1 + 2)
                sp.sem_inc(sp_passed, 1)
                sp.dma_start(a_tiles[:, bass.ds(b * QT + half * HQ, HQ), g * HG * DH:(g + 1) * HG * DH],
                             attn_sb[half][:].rearrange("p t j d -> p t (j d)")).then_inc(attn_stored[half], 16)

            for m in range(4):
                sp.wait_ge(parts_stored[m], 16 * (T // CH + 1))
            sp.wait_ge(w_cast, 3)
            for par in range(2):
                load_stacks(0, 0, range(par, len(PAIRS), 2))
                chunk_a(2 * PAIRS_LOOPED + par, PAIRS_LOOPED, par, False)
            for m in range(4):
                sp.wait_ge(parts_stored[m], 16 * (NCH + 1))
            for par in range(2):
                sp.wait_ge(v_stored[par], 16 * (NCH // 2 + 1))
            load_v(0, 0)
            load_stacks(0, 1)
            load_v(0, 1)
            load_stacks(0, 2)
            sp.wait_ge(exp_done, 3 + 1)
            load_max_rows(0)

            def group_b(b, g, b_last):
                nb, ng = (b + 1, g + 3 - NG) if g + 3 >= NG else (b, g + 3)
                if not (b_last and g + 3 >= NG):
                    sp.wait_ge(pv_done, at(b, g, NS, RING))
                    load_stacks(nb, ng)
                if not (b_last and g + 2 >= NG):
                    sp.wait_ge(v_expanded, at(b, g, 1, 1))
                    load_v(b + 1 if g + 2 >= NG else b, (g + 2) % NG)
                store_attn(b, g, b_last, 0)
                if not (b_last and g + 1 >= NG):
                    sp.wait_ge(exp_done, maxima_use(b, g, b_last) + 1 + 3)
                    load_max_rows((g + 1) % NG)
                store_attn(b, g, b_last, 1)

            with sp.Fori(0, B - 1) as b:
                for g in range(NG):
                    group_b(b, g, False)
            def load_xa(c, par):
                sp.dma_start(x_sb[par][:], x_tiles[:, bass.ds(c * TILES, TILES), :]).then_inc(xa_loaded[par], 16)
                sp.dma_start(a_sb[par][:], a_tiles[:, bass.ds(c * TILES, TILES), :]).then_inc(xa_loaded[par], 16)

            for half in range(2):
                sp.wait_ge(attn_stored[half], 16 * (NG * (B - 1) + 1))
            load_xa(0, 0)
            load_xa(1, 1)
            for g in range(NG):
                group_b(B - 1, g, True)

            for half in range(2):
                sp.wait_ge(attn_stored[half], 16 * (GROUPS + 1))

            def load_behind(c, par):
                sp.wait_ge(y_done, 2 * c + 2)
                load_xa(c + 2, par)

            def store_out(c, par):
                sp.wait_ge(out_ready, c + 1)
                sp.dma_start(out_tiles[:, bass.ds(c * TILES, TILES), :], z_sb[par][:]).then_inc(out_stored[par], 16)

            load_behind(0, 0)
            with sp.Fori(0, PAIRS_C) as i:
                load_behind(2 * i + 1, 1)
                store_out(2 * i, 0)
                load_behind(2 * i + 2, 0)
                store_out(2 * i + 1, 1)
            load_behind(NCH - 3, 1)
            for c in range(NCH - 4, NCH):
                store_out(c, c % 2)
            for par in range(2):
                sp.wait_ge(out_stored[par], 16 * (NCH // 2 + 1))

        @block.gpsimd
        def _(pool):
            pool.memset(ident[:], 0.0).then_inc(consts_ready, 1)
            pool.wait_ge(consts_ready, 1)
            pool.affine_select(out=ident[:], in_=ident[:], compare_op=ALU.not_equal, fill=1.0, base=0,
                               pattern=[[-1, P]], channel_multiplier=1).then_inc(consts_ready, 1)
            pool.memset(causal[:], 0.0).then_inc(consts_ready, 1)
            pool.memset(minus_half[:], -0.5)
            pool.wait_ge(consts_ready, 3)
            pool.affine_select(out=causal[:, T - P:T], in_=causal[:, T - P:T], compare_op=ALU.is_ge, fill=LOWEST,
                               base=0, pattern=[[-1, P]], channel_multiplier=1).then_inc(consts_ready, 1)
            pool.tensor_copy(ident_bf[:], ident[:]).then_inc(consts_ready, 1)
            pool.tensor_copy(ident_f16[:], ident[:]).then_inc(consts_ready, 1)
            pool.wait_ge(consts_ready, 6)
            for k, (name, n_, b_) in enumerate((("gate", wgate_n, wgate_b), ("up", wup_n, wup_b),
                                                ("down", wdown_n, wdown_b))):
                pool.wait_ge(w_loaded[name], 16)
                pool.tensor_copy(b_[:], n_[:]).then_inc(w_cast, 1)
                pool.wait_ge(w_cast, k + 1)
            for i in range(2):
                pool.memset(v_ones[i][:, :, :, DH:32], 1.0).then_inc(preset, 1)
                pool.wait_ge(preset, i + 1)
            for g in range(4):
                pool.memset(k_stack[g][ROWS:ROWS_M, :, :], -1.0).then_inc(preset, 1)
                pool.wait_ge(preset, 2 + g + 1)

            def inverse_deviation(ln, step, c):
                pool.wait_ge(step, 3 * c + 3)
                pool.tensor_tensor(rstd[:, ln, :], var_eps[:, ln, :], minus_half[:],
                                   ALU.pow).then_inc(rstd_done[ln], 1)

            def expand_v(b, g):
                pool.wait_ge(v_loaded[g % 2], 16 * (2 * b + g // 2 + 1))
                pool.sem_inc(pool_passed, 1)
                pool.tensor_copy(v_ones[g % 2][:, :, :, 0:DH],
                                 v_flat[g % 2][:].rearrange("p t (j d) -> p t j d", j=HG)).then_inc(v_expanded, 1)

            expand_v(0, 0)

            def mask(s, uses):
                pool.wait_ge(exp_done, uses + 3)
                pool.sem_inc(pool_passed, 1)
                tile = probs[s % RING][:, :, 0:P]
                pool.affine_select(out=tile, in_=tile, compare_op=ALU.is_ge, fill=0.0, base=0,
                                   pattern=[[0, HG], [1, P]], channel_multiplier=-1).then_inc(masked, 1)

            for s in range(AHEAD):
                mask(s, bank_use(0, 0, False, HG * s + HG - 1) + 1)

            def group_b(b, g, b_last):
                last_group = b_last and g == NG - 1
                for d, s in enumerate(s for s in range(AHEAD, NS if last_group else NS + AHEAD) if s % NS in diagonal):
                    if d == 1 and not last_group:
                        pool.wait_ge(pv_done, at(b, g, NS, RING))
                        expand_v(b + 1 if g == NG - 1 else b, (g + 1) % NG)
                    mask(s, bank_use(b, g, b_last, HG * s + HG - 1) + 1)
                    if last_group and s == HQ - 1:
                        inverse_deviation(0, ln1_step, 0)

            with pool.Fori(0, B - 1) as b:
                for g in range(NG):
                    group_b(b, g, False)
            for g in range(NG):
                group_b(B - 1, g, True)

            pool.sem_inc(h_lo_done, 3)

            def chunk_c(c, has_prev, has_next):
                for hc in range(HC):
                    if hc == 2 and has_next:
                        inverse_deviation(0, ln1_step, c + 1)
                    pool.wait_ge(h_hi_done, HC * c + hc + 1)
                    pool.tensor_tensor(h_lo[:, hc, :], h_sb[hc % 3][:], h_hi[:, hc, :],
                                       ALU.subtract).then_inc(h_lo_done, 1)
                if has_prev:
                    inverse_deviation(1, ln2_step, c - 1)

            chunk_c(0, False, True)
            with pool.Fori(1, NCH - 1) as c:
                chunk_c(c, True, True)
            chunk_c(NCH - 1, True, False)
            inverse_deviation(1, ln2_step, NCH - 1)

        @block.scalar
        def _(act):
            for u in range(0, len(early_units), 2):
                act.wait_ge(wt_ready, u + 1)
                act.copy(early_units[u][2], unit_bank(early_units[u], u)).then_inc(wt_copied[0], 1)

            act.sem_inc(xt_copied[0], 1)
            act.sem_inc(part1_done, 2)
            act.sem_inc(v_copied[0], 1)
            for m in range(4):
                act.sem_inc(parts_stored[m], 16)

            def copy_xt(c, par):
                act.wait_ge(xt_ready, 2 * c + 1)
                act.wait_ge(v_ready, 2 * c + 2)
                act.copy(x_t[par][:, 0, :], ps[:, 0, :]).then_inc(xt_copied[0], 1)

            def part0(c, m):
                act.wait_ge(qk_ready, 4 * c + m + 1)
                act.wait_ge(parts_stored[m], 16 * c + 16)
                act.copy(parts[m][:, 0, :], ps[:, 2 + m, :]).then_inc(part0_done, 1)

            def part1(c, m):
                act.wait_ge(qk_bank_free, 4 * c + 4 + m + 1)
                act.copy(parts[m][:, 1, :], rest[m % 2][:]).then_inc(part1_done, 1)

            def chunk_a(c, i, par, has_next):
                if has_next:
                    copy_xt(c + 1, 1 - par)
                part0(c, 0)
                part0(c, 1)
                part1(c, 0)
                part0(c, 2)
                part1(c, 1)
                part0(c, 3)
                part1(c, 2)
                part1(c, 3)
                act.wait_ge(v_ready, 2 * c + 4 + 1)
                act.wait_ge(v_stored[par], 16 * i + 16)
                act.copy(v_sb[par][:, 0:2, :].rearrange("p t d -> p (t d)"), ps[:, 6, :]).then_inc(v_copied[0], 1)

            copy_xt(0, 0)
            with act.Fori(0, PAIRS_LOOPED) as i:
                for par in range(2):
                    chunk_a(2 * i + par, i, par, True)
            for par in range(2):
                chunk_a(2 * PAIRS_LOOPED + par, PAIRS_LOOPED, par, par == 0)

            act.sem_inc(exp_done, 3)
            act.sem_inc(o_copied, 1)

            def copy_max_rows(turned, bank):
                act.wait_ge(max_turned, turned)
                act.copy(max_rows[:], bank_bf(bank)[0:3 * NM, 0:P]).then_inc(exp_done, 1)

            for u, unit in enumerate(late_units):
                act.wait_ge(late_wt_ready, u + 1)
                act.copy(unit[2], unit_bank(unit, 4 + u % 4)).then_inc(late_wt_copied, 1)
            copy_max_rows(1, 4)

            def exponential(n, st, pv):
                s, j = divmod(n, HG)
                w = slots[s % NS][2] * P
                act.wait_ge(st_ready, st + 1)
                if j == 0:
                    act.wait_ge(pv_done, pv)
                act.activation(probs[s % RING][:, j, 0:w], ps[:, 4 + n % 3, 0:w], ACT.Exp,
                               scale=SOFT_SCALE).then_inc(exp_done, 1)

            for n in range(HG * AHEAD):
                exponential(n, n, n // HG + 1)

            def group_b(b, g, b_last):
                def copy_o(half):
                    act.wait_ge(pv_done, at(b, g, NS, RING + HALF_END[half] + 1))
                    act.wait_ge(recip_done, at(b, g, 2, 1 + half))
                    act.copy(o_sb[:], ps[:, 7, :]).then_inc(o_copied, 1)

                for step in group_steps(b_last, g):
                    if step[0] == "st":
                        _, s, j = step
                        exponential(HG * s + j, at(b, g, NE, HG * s + j), at(b, g, NS, s + 1))
                    elif step[0] == "oC":
                        copy_o(step[1])
                    elif step[0] == "mT":
                        act.wait_ge(max_rows_loaded, at(b, g, 48, 48))
                        copy_max_rows(at(b, g, 1, 2), 4 + maxima_at(b_last, g) % 3)

            def copy_at(c):
                act.wait_ge(at_ready, 2 * c + 1)
                act.wait_ge(proj_ready, 2 * c + 2)
                act.copy(a_t[:, 0, :], ps[:, 0, :]).then_inc(at_copied[0], 1)

            with act.Fori(0, B - 1) as b:
                for g in range(NG):
                    group_b(b, g, False)
            for g in range(NG):
                if g == NG - 1:
                    copy_at(0)
                group_b(B - 1, g, True)

            def split_x1(c, par):
                act.wait_ge(x1_ready, c + 1)
                act.copy(x1_hi_rows[:], x1[par][:]).then_inc(x1_hi_split, 1)

            def x1_high(c):
                act.wait_ge(x1t_ready[0], c + 1)
                act.copy(x1_hi[:], bank_f16(0)).then_inc(x1_done[0], 1)

            def chunk_c(c, par, has_next):
                for hc in range(HC + 1):
                    if hc < HC:
                        act.wait_ge(gate_ready, HC * c + hc + 1)
                        act.wait_ge(h_done, HC * c + hc + 1)
                        act.activation(silu[hc % 2][:], ps[:, 4 + 2 * (hc % 2), :], ACT.Silu,
                                       scale=W_SCALE).then_inc(silu_done, 1)
                    if hc == HC - 1 and has_next:
                        split_x1(c + 1, 1 - par)
                    if hc >= 1:
                        if hc == 1:
                            act.wait_ge(down_ready, 2 * c + 2)
                        act.wait_ge(h_done, HC * c + 2 + hc)
                        act.copy(h_hi[:, hc - 1, :], h_sb[(hc - 1) % 3][:]).then_inc(h_hi_done, 1)

            split_x1(0, 0)
            x1_high(0)
            copy_at(1)
            with act.Fori(0, PAIRS_LOOPED) as i:
                for par in range(2):
                    chunk_c(2 * i + par, par, True)
                    x1_high(2 * i + par + 1)
                    copy_at(2 * i + par + 2)
            chunk_c(NCH - 2, 0, True)
            x1_high(NCH - 1)
            chunk_c(NCH - 1, 1, False)

        @block.vector
        def _(dve):
            for u in range(1, len(early_units), 2):
                dve.wait_ge(wt_ready, u + 1)
                dve.tensor_copy(early_units[u][2], unit_bank(early_units[u], u)).then_inc(wt_copied[1], 1)

            dve.sem_inc(xt_copied[1], 1)
            dve.sem_inc(qk_bank_free, 4)
            dve.sem_inc(part2_done, 2)
            dve.sem_inc(v_copied[1], 1)
            for par in range(2):
                dve.sem_inc(v_stored[par], 16)

            def copy_xt(c, par):
                dve.wait_ge(xt_ready, 2 * c + 2)
                dve.wait_ge(v_ready, 2 * c + 2)
                dve.tensor_copy(x_t[par][:, 1, :], ps[:, 1, :]).then_inc(xt_copied[1], 1)

            def rest_of(c, m):
                dve.wait_ge(part0_done, 4 * c + m + 1)
                dve.wait_ge(part1_done, 4 * c + m + 1)
                dve.wait_ge(part2_done, 4 * c + m + 1)
                dve.tensor_tensor(rest[m % 2][:], ps[:, 2 + m, :], parts[m][:, 0, :],
                                  ALU.subtract).then_inc(qk_bank_free, 1)

            def part2(c, m):
                dve.wait_ge(part1_done, 4 * c + 2 + m + 1)
                dve.tensor_tensor(parts[m][:, 2, :], rest[m % 2][:], parts[m][:, 1, :],
                                  ALU.subtract).then_inc(part2_done, 1)

            def chunk_a(c, i, par, has_next):
                if has_next:
                    copy_xt(c + 1, 1 - par)
                rest_of(c, 0)
                rest_of(c, 1)
                part2(c, 0)
                rest_of(c, 2)
                part2(c, 1)
                rest_of(c, 3)
                part2(c, 2)
                part2(c, 3)
                dve.wait_ge(v_ready, 2 * c + 4 + 2)
                dve.wait_ge(v_stored[par], 16 * i + 16)
                dve.tensor_copy(v_sb[par][:, 2:4, :].rearrange("p t d -> p (t d)"),
                                ps[:, 7, :]).then_inc(v_copied[1], 1)

            copy_xt(0, 0)
            with dve.Fori(0, PAIRS_LOOPED) as i:
                for par in range(2):
                    chunk_a(2 * i + par, i, par, True)
            for par in range(2):
                chunk_a(2 * PAIRS_LOOPED + par, PAIRS_LOOPED, par, par == 0)

            dve.sem_inc(s_free, 2)
            dve.sem_inc(recip_done, 1)
            for half in range(2):
                dve.sem_inc(attn_stored[half], 16)
            dve.wait_ge(consts_ready, 6)

            def row_maxima(use, pair, u):
                dve.wait_ge(s_ready, use + 1)
                dve.sem_inc(dve_passed, 1)
                k0 = 0
                for j, qt in max_units[u % NU]:
                    w = (qt + 1) * P
                    scores = ps[:, 2 * pair:2 * pair + 2, :].rearrange("p a b -> p (a b)")[:, k0:k0 + w]
                    last = dve.tensor_tensor_reduce(scores, scores, causal[:, T - w:T], 1.0, LOWEST, ALU.add, ALU.max,
                                                    row_max[:, j * QT + qt:j * QT + qt + 1])
                    k0 += w
                last.then_inc(s_free, 1)

            def split_max(count, uses, first=False):
                dve.wait_ge(s_free, uses + 2)
                if not first:
                    dve.wait_ge(max_turned, count)
                dve.tensor_copy(max_parts[:, 0, :], row_max[:]).then_inc(max_step, 1)
                dve.wait_ge(max_step, 4 * count + 1)
                dve.tensor_tensor(max_rest[:, 0, :], row_max[:], max_parts[:, 0, :], ALU.subtract).then_inc(max_step, 1)
                dve.wait_ge(max_step, 4 * count + 2)
                dve.tensor_copy(max_parts[:, 1, :], max_rest[:, 0, :]).then_inc(max_step, 1)
                dve.wait_ge(max_step, 4 * count + 3)
                dve.tensor_tensor(max_rest[:, 1, :], max_rest[:, 0, :], max_parts[:, 1, :], ALU.subtract).then_inc(max_step, 1)
                dve.wait_ge(max_step, 4 * count + 4)
                dve.tensor_copy(max_parts[:, 2, :], max_rest[:, 1, :]).then_inc(max_parts_ready, 1)

            for u in range(NU + UNITS_AHEAD):
                row_maxima(u, u % 2, u)
                if u == NU - 1:
                    split_max(0, NU, True)

            def group_b(b, g, b_last):
                def normalise(use, pair, half):
                    turned = ps[:, 2 * pair, :].rearrange("p (t j e) -> p t j e", t=HQ, j=HG)
                    dve.wait_ge(s_ready, use + 1)
                    dve.reciprocal(recip[:, half], turned[:, :, :, DH]).then_inc(recip_done, 1)
                    dve.wait_ge(recip_done, at(b, g, 2, 1 + half + 1))
                    dve.wait_ge(attn_stored[half], at(b, g, 16, 16))
                    dve.tensor_tensor(attn_sb[half][:], turned[:, :, :, 0:DH],
                                      recip[:, half].unsqueeze(3).to_broadcast([P, HQ, HG, DH]),
                                      ALU.mult).then_inc(s_free, 1)

                for step in group_steps(b_last, g):
                    if step[0] == "max":
                        use, pair = pair_use(b, g, b_last, step)
                        row_maxima(use, pair, step[1])
                        if step[1] == NU - 1:
                            split_max(at(b, g, 1, 1), use + 1)
                    elif step[0] == "oT":
                        normalise(*pair_use(b, g, b_last, step), step[1])

            def copy_at(c):
                dve.wait_ge(at_ready, 2 * c + 2)
                dve.wait_ge(proj_ready, 2 * c + 2)
                dve.tensor_copy(a_t[:, 1, :], ps[:, 1, :]).then_inc(at_copied[1], 1)

            def y_bank(c, i, par, k):
                if k == 0:
                    dve.wait_ge(xa_loaded[par], 32 * i + 32)
                dve.wait_ge(proj_ready, 2 * c + 2 + k + 1)
                dve.tensor_tensor(x1[par][:, 2 * k:2 * k + 2, :].rearrange("p t d -> p (t d)"), ps[:, 2 + k, :],
                                  x_sb[par][:, 2 * k:2 * k + 2, :].rearrange("p t d -> p (t d)"),
                                  ALU.add).then_inc(y_done, 1)

            def ln_stats(ln, step, c, buf, tiles):
                for t in tiles:
                    last = dve.bn_stats(stats[:, ln, t, :], buf[:, t, :])
                if TILES - 1 in tiles:
                    last.then_inc(step, 1)

            def ln_variance(ln, step, c):
                dve.wait_ge(step, 3 * c + 1)
                dve.sem_inc(dve_passed, 1)
                for t in range(TILES):
                    last = dve.bn_aggr(mean_var[:, ln, t, :], stats[:, ln, t, :])
                last.then_inc(step, 1)
                dve.wait_ge(step, 3 * c + 2)
                dve.tensor_scalar(var_eps[:, ln, :], mean_var[:, ln, :, 1], EPS, None, ALU.add).then_inc(step, 1)

            def ln_apply(ln, c, buf, done):
                dve.wait_ge(rstd_done[ln], c + 1)
                for t in range(TILES):
                    last = dve.tensor_scalar(buf[:, t, :], buf[:, t, :], mean_var[:, ln, t, 0:1],
                                             rstd[:, ln, t:t + 1], ALU.subtract, ALU.mult)
                last.then_inc(done, 1)

            with dve.Fori(0, B - 1) as b:
                for g in range(NG):
                    group_b(b, g, False)
            for g in range(NG):
                if g == NG - 1:
                    copy_at(0)
                    y_bank(0, 0, 0, 0)
                    y_bank(0, 0, 0, 1)
                    dve.wait_ge(y_done, 2)
                    ln_stats(0, ln1_step, 0, x1[0], range(TILES))
                    ln_variance(0, ln1_step, 0)
                    ln_apply(0, 0, x1[0], x1_ready)
                group_b(B - 1, g, True)

            dve.sem_inc(h_done, 2)
            dve.sem_inc(z_done, 2)
            for par in range(2):
                dve.sem_inc(out_stored[par], 16)

            def z_banks(c, i, par):
                for k in range(2):
                    dve.wait_ge(down_ready, 2 * c + 2 + k + 1)
                    if k == 0:
                        dve.wait_ge(out_stored[par], 16 * i + 16)
                    dve.scalar_tensor_tensor(out=z_sb[par][:, 2 * k:2 * k + 2, :].rearrange("p t d -> p (t d)"),
                                             in0=ps[:, 2 + k, :], scalar=2.0 * W_SCALE,
                                             in1=x1[par][:, 2 * k:2 * k + 2, :].rearrange("p t d -> p (t d)"),
                                             op0=ALU.mult, op1=ALU.add).then_inc(z_done, 1)

            def split_x1(c, par):
                dve.wait_ge(x1_hi_split, c + 1)
                dve.tensor_tensor(x1_lo_rows[:], x1[par][:], x1_hi_rows[:], ALU.subtract).then_inc(x1_lo_split, 1)

            def x1_low(c):
                dve.wait_ge(x1t_ready[1], c + 1)
                dve.tensor_copy(x1_lo[:], bank_f16(1)).then_inc(x1_done[1], 1)

            def hidden(c, hc):
                dve.wait_ge(silu_done, HC * c + hc + 1)
                dve.wait_ge(up_ready, HC * c + hc + 1)
                dve.wait_ge(h_lo_done, HC * c + hc + 1)
                dve.scalar_tensor_tensor(out=h_sb[hc % 3][:], in0=ps[:, 5 + 2 * (hc % 2), :], scalar=0.5 * W_SCALE,
                                         in1=silu[hc % 2][:], op0=ALU.mult, op1=ALU.mult).then_inc(h_done, 1)

            def chunk_c(c, i, par, has_prev, has_next, has_third):
                n, ni, npar = c + 1, i + par, 1 - par
                if has_prev:
                    z_banks(c - 1, i + par - 1, npar)
                hidden(c, 0)
                if has_next:
                    y_bank(n, ni, npar, 0)
                    y_bank(n, ni, npar, 1)
                hidden(c, 1)
                if has_next:
                    dve.wait_ge(y_done, 2 * n + 2)
                    ln_stats(0, ln1_step, n, x1[npar], range(TILES))
                    ln_variance(0, ln1_step, n)
                hidden(c, 2)
                hidden(c, 3)
                if has_next:
                    ln_apply(0, n, x1[npar], x1_ready)
                hidden(c, 4)
                hidden(c, 5)
                if has_next:
                    split_x1(n, npar)
                if has_prev:
                    dve.wait_ge(z_done, 2 * c + 2)
                    ln_stats(1, ln2_step, c - 1, z_sb[npar], range(TILES))
                    ln_variance(1, ln2_step, c - 1)
                if has_next:
                    x1_low(n)
                if has_prev:
                    ln_apply(1, c - 1, z_sb[npar], out_ready)
                if has_third:
                    copy_at(c + 2)

            split_x1(0, 0)
            x1_low(0)
            copy_at(1)
            chunk_c(0, 0, 0, False, True, True)
            with dve.Fori(0, PAIRS_C) as i:
                chunk_c(2 * i + 1, i, 1, True, True, True)
                chunk_c(2 * i + 2, i + 1, 0, True, True, True)
            for c in range(NCH - 3, NCH):
                chunk_c(c, c // 2, c % 2, True, c < NCH - 1, c < NCH - 2)
            z_banks(NCH - 1, PAIRS_LOOPED, 1)
            dve.wait_ge(z_done, 2 * NCH + 2)
            ln_stats(1, ln2_step, NCH - 1, z_sb[1], range(TILES))
            ln_variance(1, ln2_step, NCH - 1)
            ln_apply(1, NCH - 1, z_sb[1], out_ready)

        @block.tensor
        def _(pe):
            def turn_weights(unit, b, ready):
                name, tiles, dst = unit
                for n, tile in enumerate(tiles):
                    last = pe.transpose(unit_bank(unit, b)[:, tile_cols(n)], tile,
                                        ident_bf[:] if name in casts else ident[:])
                last.then_inc(ready, 1)

            pe.wait_ge(consts_ready, 2)
            pe.wait_ge(w_loaded["qkv"], 16)
            for u, unit in enumerate(early_units):
                turn_weights(unit, u, wt_ready)
            pe.wait_ge(wt_copied[0], (len(early_units) + 1) // 2)
            pe.wait_ge(wt_copied[1], len(early_units) // 2)

            pe.sem_inc(v_ready, 4)

            def turn_x(c, i, par):
                pe.wait_ge(x_loaded[par], 16 * i + 16)
                for kc in range(KC):
                    pe.wait_ge(xt_copied[kc], c + 1)
                    for t in range(TILES):
                        last = pe.transpose(ps[:, kc, tile_cols(t)], x_sb[par][:, t, kc * P:(kc + 1) * P], ident[:])
                    last.then_inc(xt_ready, 1)

            def chunk_a(c, i, par, has_next):
                if has_next:
                    turn_x(c + 1, i + par, 1 - par)
                pe.wait_ge(xt_copied[0], c + 2)
                pe.wait_ge(xt_copied[1], c + 2)
                for m in range(4):
                    pe.wait_ge(qk_bank_free, 4 * c + m + 1)
                    for kc in range(KC):
                        last = pe.matmul(ps[:, 2 + m, :], wqkv_t[:, kc, m * P:(m + 1) * P], x_t[par][:, kc, :],
                                         start=kc == 0, stop=kc == KC - 1)
                    last.then_inc(qk_ready, 1)
                for k in range(2):
                    pe.wait_ge(v_copied[k], c + 1)
                    for t in (2 * k, 2 * k + 1):
                        for kc in range(KC):
                            last = pe.matmul(ps[:, 6 + k, (t % 2) * D:(t % 2 + 1) * D], x_t[par][:, kc, tile_cols(t)],
                                             wqkv_t[:, kc, 2 * D:3 * D], start=kc == 0, stop=kc == KC - 1)
                    last.then_inc(v_ready, 1)

            turn_x(0, 0, 0)
            with pe.Fori(0, PAIRS_LOOPED) as i:
                for par in range(2):
                    chunk_a(2 * i + par, i, par, True)
            for par in range(2):
                chunk_a(2 * PAIRS_LOOPED + par, PAIRS_LOOPED, par, par == 0)
            for k in range(2):
                pe.wait_ge(xt_copied[k], NCH + 1)
                pe.wait_ge(v_copied[k], NCH + 1)
            pe.wait_ge(qk_bank_free, 4 * NCH + 4)

            pe.wait_ge(preset, 6)

            pe.sem_inc(pv_done, RING)
            pe.sem_inc(proj_ready, 2)

            def scores_for_max(g, use, pair, u):
                pe.wait_ge(s_free, use + 1)
                c0 = 0
                for j, qt in max_units[u % NU]:
                    k0, k_end = 0, (qt + 1) * P
                    while k0 < k_end:
                        w = min(CH - c0 % CH, k_end - k0)
                        last = pe.matmul(ps[:, 2 * pair + c0 // CH, c0 % CH:c0 % CH + w],
                                         q_stack[g][0:ROWS, j, tile_cols(qt)], k_stack[g][0:ROWS, j, k0:k0 + w],
                                         start=True, stop=True)
                        k0, c0 = k0 + w, c0 + w
                last.then_inc(s_ready, 1)

            def turn_max(ready, bank):
                pe.wait_ge(max_parts_ready, ready)
                pe.transpose(bank_bf(bank)[0:3 * NM, 0:P], max_parts[:].rearrange("p a m -> p (a m)"),
                             ident_bf[:]).then_inc(max_turned, 1)

            def scores(g, n, before):
                s, j = divmod(n, HG)
                half, kt, w = slots[s]
                q0 = max(half * HQ, kt) * P
                pe.wait_ge(exp_done, before + 1 + 3)
                pe.matmul(ps[:, 4 + n % 3, 0:w * P], k_stack[g][0:ROWS_M, j, tile_cols(kt)],
                          q_stack[g][0:ROWS_M, j, q0:q0 + w * P], start=True, stop=True).then_inc(st_ready, 1)

            first_scores = NU + UNITS_AHEAD - HG * AHEAD
            for u in range(NU + UNITS_AHEAD):
                if u % NU == 0:
                    pe.wait_ge(stack_loaded[u // NU], 16 * 12)
                scores_for_max(u // NU, u, u % 2, u)
                if u < len(late_units):
                    name = late_units[u][0]
                    pe.wait_ge(w_loaded[name], 16)
                    if name in casts:
                        pe.wait_ge(w_cast, casts[name])
                        pe.wait_ge(consts_ready, 5)
                    if u >= 4:
                        pe.wait_ge(late_wt_copied, u - 3)
                    turn_weights(late_units[u], 4 + u % 4, late_wt_ready)
                if u == NU + 1:
                    pe.wait_ge(late_wt_copied, len(late_units))
                    turn_max(1, 4)
                if u >= first_scores:
                    n = u - first_scores
                    if n == 0:
                        pe.wait_ge(max_rows_loaded, 48)
                    scores(0, n, bank_use(0, 0, False, n - 3))


            def turn_attn(c, i, par, first=False):
                pe.wait_ge(xa_loaded[par], 32 * i + 32)
                if not first:
                    pe.wait_ge(x1_done[0], c)
                    pe.wait_ge(x1_done[1], c)
                for kc in range(KC):
                    for t in range(TILES):
                        last = pe.transpose(ps[:, kc, tile_cols(t)], a_sb[par][:, t, kc * P:(kc + 1) * P], ident[:])
                    last.then_inc(at_ready, 1)

            def project(c, tiles=range(TILES)):
                pe.wait_ge(at_copied[0], c + 1)
                pe.wait_ge(at_copied[1], c + 1)
                for t in tiles:
                    for kc in range(KC):
                        last = pe.matmul(ps[:, 2 + t // 2, (t % 2) * D:(t % 2 + 1) * D], a_t[:, kc, tile_cols(t)],
                                         wproj_t[:, kc, :], start=kc == 0, stop=kc == KC - 1)
                    if t % 2:
                        last.then_inc(proj_ready, 1)

            def group_b(b, g, b_last):
                for k, step in enumerate(group_steps(b_last, g)):
                    if b_last and g == NG - 1 and k in (6, 14):
                        project(0, (0, 1) if k == 6 else (2, 3))
                    if step[0] == "st":
                        _, s, j = step
                        if s == NS and j == 0:
                            pe.wait_ge(max_rows_loaded, at(b, g, 48, 96))
                        n = HG * s + j
                        scores((g + s // NS) % NG, n % NE, maxima_use(b, g, b_last) if n == maxima_at(b_last, g)
                               else bank_use(b, g, b_last, n - 3))
                    elif step[0] == "pv":
                        s = step[1]
                        half, kt, w = slots[s]
                        c0 = (max(half * HQ, kt) - half * HQ) * P
                        if s == 0:
                            pe.wait_ge(v_expanded, at(b, g, 1, 1))
                        if kt == 0:
                            pe.wait_ge(o_copied, at(b, g, 2, 1 + half))
                        if s in diagonal:
                            pe.wait_ge(masked, at(b, g, ND, diagonal.index(s) + 1))
                        else:
                            pe.wait_ge(exp_done, bank_use(b, g, b_last, HG * s + HG - 1) + 1 + 3)
                        for j in range(HG):
                            last = pe.matmul(ps[32 * j:32 * j + 32, 7, c0:c0 + w * P], v_ones[g % 2][:, kt, j, :],
                                             probs[s % RING][:, j, 0:w * P], start=kt == 0, stop=s == HALF_END[half])
                        last.then_inc(pv_done, 1)
                    elif step[0] == "max":
                        if step[1] == NU:
                            pe.wait_ge(stack_loaded[(g + 2) % NG], 192 * (b + (g + 2) // NG + 1))
                        scores_for_max((g + 1 + step[1] // NU) % NG, *pair_use(b, g, b_last, step), step[1])
                    elif step[0] == "mT":
                        n = maxima_at(b_last, g)
                        pe.wait_ge(exp_done, bank_use(b, g, b_last, n - 3) + 1 + 3)
                        turn_max(at(b, g, 1, 2), 4 + n % 3)
                    elif step[0] == "oT":
                        half = step[1]
                        pe.wait_ge(o_copied, at(b, g, 2, 1 + half + 1))
                        use, pair = pair_use(b, g, b_last, step)
                        pe.wait_ge(s_free, use + 1)
                        if b_last and g == NG - 1:
                            pe.wait_ge(y_done, 2)
                        for t in range(HQ):
                            last = pe.transpose(ps[:, 2 * pair, tile_cols(t)], o_sb[:, tile_cols(t)], ident[:])
                        last.then_inc(s_ready, 1)

            with pe.Fori(0, B - 1) as b:
                for g in range(NG):
                    group_b(b, g, False)
            for g in range(NG):
                if g == NG - 1:
                    pe.wait_ge(s_free, 2 + pair_use(B - 1, g, True, ("oT", 0))[0])
                    turn_attn(0, 0, 0, first=True)
                group_b(B - 1, g, True)
            pe.wait_ge(s_free, 2 + NP * GROUPS)
            pe.wait_ge(exp_done, 3 + NR * GROUPS)
            pe.wait_ge(o_copied, 1 + 2 * GROUPS)

            pe.sem_inc(down_ready, 2)

            def turn_x1(c, part):
                rows, split = ((x1_hi_rows, x1_hi_split), (x1_lo_rows, x1_lo_split))[part]
                pe.wait_ge(split, c + 1)
                for kc in range(KC):
                    for t in range(TILES):
                        last = pe.transpose(bank_f16(part)[:, kc, tile_cols(t)], rows[:, t, kc * P:(kc + 1) * P],
                                            ident_f16[:])
                last.then_inc(x1t_ready[part], 1)

            def chunk_c(c, i, par, has_next, has_third):
                for part in range(2):
                    pe.wait_ge(x1_done[part], c + 1)
                for hc in range(HC):
                    if hc == 1 and has_next:
                        pe.wait_ge(z_done, 2 * c + 2)
                        project(c + 1)
                    pe.wait_ge(h_done, HC * c + hc + 1)
                    for w, bank, ready in ((wgate_t, 4, gate_ready), (wup_t, 5, up_ready)):
                        for kc in range(KC):
                            for part in (x1_hi, x1_lo):
                                last = pe.matmul(ps[:, bank + 2 * (hc % 2), :], w[:, kc, hc * P:(hc + 1) * P], part[:, kc, :],
                                                 start=kc == 0 and part is x1_hi, stop=kc == KC - 1 and part is x1_lo)
                        last.then_inc(ready, 1)
                if has_next:
                    pe.wait_ge(y_done, 2 * c + 4)
                for hc in range(HC):
                    if hc in (TURN_HI, TURN_LO) and has_next:
                        turn_x1(c + 1, (TURN_HI, TURN_LO).index(hc))
                    if hc == 5 and has_third:
                        turn_attn(c + 2, i + 1, par)
                    pe.wait_ge(h_lo_done, HC * c + 3 + hc + 1)
                    for t in range(TILES):
                        for part in (h_hi, h_lo):
                            last = pe.matmul(ps[:, 2 + t // 2, (t % 2) * D:(t % 2 + 1) * D], part[:, hc, tile_cols(t)],
                                             wdown_t[:, hc, :], start=hc == 0 and part is h_hi and t % 2 == 0,
                                             stop=hc == HC - 1 and part is h_lo, skip_group_check=True)
                        if hc == HC - 1 and t % 2:
                            last.then_inc(down_ready, 1)

            turn_x1(0, 0)
            turn_x1(0, 1)
            turn_attn(1, 0, 1)
            chunk_c(0, 0, 0, True, True)
            with pe.Fori(0, PAIRS_C) as i:
                chunk_c(2 * i + 1, i, 1, True, True)
                chunk_c(2 * i + 2, i + 1, 0, True, True)
            for c in range(NCH - 3, NCH):
                chunk_c(c, c // 2, c % 2, c < NCH - 1, c < NCH - 2)


_INS = ["L0_attn_x", "L0_attn_W_qkv", "L0_attn_W_proj", "L0_ffn_w_gate", "L0_ffn_w_up", "L0_ffn_w_down"]


def kernel(**inputs):
    import numpy as _np
    import concourse.bacc as _bacc
    from concourse import mybir as _mybir
    from concourse.bass_utils import run_bass_kernel_spmd as _run

    nc = _bacc.Bacc("TRN2", target_bir_lowering=False, num_devices=1)
    arrays, args = {}, []
    for name in _INS:
        a = _np.ascontiguousarray(inputs[name])
        arrays[f"in_{name}"] = a
        args.append(nc.dram_tensor(f"in_{name}", a.shape, _mybir.dt.from_np(a.dtype), kind="ExternalInput").ap())
    out = nc.dram_tensor("out_x", inputs["L0_attn_x"].shape, F32, kind="ExternalOutput").ap()
    block_kernel(nc, *args, out)
    r = _run(nc, [arrays], core_ids=[0])
    return r.results[0]["out_x"]
```
